# Optimizing a Trainium2 kernel written in Bass

```python
import numpy as np
import jax
import jax.numpy as jnp

def _softmax(x, axis=-1):
    return jax.nn.softmax(x, axis=axis)

def _gelu(x):
    return jax.nn.gelu(x, approximate=True)

def _silu(x):
    return jax.nn.silu(x)

def _sigmoid(x):
    return jax.nn.sigmoid(x)

def _layernorm(x, axis=-1, eps=1e-05):
    m = jnp.mean(x, axis=axis, keepdims=True)
    v = jnp.var(x, axis=axis, keepdims=True)
    return (x - m) / jnp.sqrt(v + eps)

def _scatter_add(tgt, idx, src, axis=0):
    return tgt.at[idx].add(src)

def _segment_sum(src, seg, n):
    return jax.ops.segment_sum(src, seg, n)
kernel_name = 'mk_conv_preact_d2_conv_nchw512_r4_bf2af3'

def setup_inputs(seed: int=0):
    np.random.seed(seed)
    _w = jnp.asarray

    def _rec_inputs():
        import jax
        import jax.numpy as jnp
        _gk = jax.random.key(seed)
        x = -0.0003929 + 0.9999 * jax.random.normal(jax.random.fold_in(_gk, 1), (8, 128, 16, 16), jnp.float32)
        return x
    x = _rec_inputs()

    def _L0_conv_setup():
        import jax, jax.numpy as jnp
        import numpy as np
        DIM = 128
        HEADS = 8
        HEAD_DIM = DIM // HEADS
        SCALE = HEAD_DIM ** (-0.5)
        B, H, W = (8, 16, 16)

        def rotate_every_two(x):
            x1 = x[..., ::2]
            x2 = x[..., 1::2]
            return jnp.stack([-x2, x1], axis=-1).reshape(x.shape)

        def theta_shift(x, sin, cos):
            return x * cos + rotate_every_two(x) * sin
        key = jax.random.key(seed)
        ks = jax.random.split(key, 6)
        N = H * W
        x = jax.random.normal(ks[0], (B, DIM, H, W), jnp.float32)
        sin = jax.random.uniform(ks[1], (N, HEAD_DIM), jnp.float32, minval=-1.0, maxval=1.0)
        cos = jax.random.uniform(ks[2], (N, HEAD_DIM), jnp.float32, minval=-1.0, maxval=1.0)
        w_qkvo = jax.random.normal(ks[3], (4 * DIM, DIM), jnp.float32) * DIM ** (-0.5)
        b_qkvo = jnp.zeros((4 * DIM,), jnp.float32)
        w_lepe = jax.random.normal(ks[4], (DIM, 1, 5, 5), jnp.float32) * 0.1
        b_lepe = jnp.zeros((DIM,), jnp.float32)
        w_proj = jax.random.normal(ks[5], (DIM, DIM), jnp.float32) * DIM ** (-0.5)
        b_proj = jnp.zeros((DIM,), jnp.float32)
        return dict(x=x, sin=sin, cos=cos, w_qkvo=w_qkvo, b_qkvo=b_qkvo, w_lepe=w_lepe, b_lepe=b_lepe, w_proj=w_proj, b_proj=b_proj)
    _L0_conv_all = _L0_conv_setup()
    _L0_conv_in = {k: v for k, v in _L0_conv_all.items() if k in ('sin', 'cos', 'w_qkvo', 'b_qkvo', 'w_lepe', 'b_lepe', 'w_proj', 'b_proj')}
    del _L0_conv_all

    def _L1_conv_setup():
        import jax, jax.numpy as jnp
        import numpy as np
        INPUT_DIM = 128
        OUTPUT_DIM = 128
        D_STATE = 16
        D_CONV = 4
        EXPAND = 2
        D_MODEL = INPUT_DIM // 4
        D_INNER = EXPAND * D_MODEL
        DT_RANK = (D_MODEL + 15) // 16

        def layernorm(x, w, b, eps=1e-05):
            mu = jnp.mean(x, axis=-1, keepdims=True)
            var = jnp.var(x, axis=-1, keepdims=True)
            return (x - mu) * jax.lax.rsqrt(var + eps) * w + b

        def selective_scan(u, delta, A, Bm, Cm, Dp):
            N, L, d = u.shape
            s = A.shape[1]

            def step(h, inp):
                u_t, d_t, B_t, C_t = inp
                h = jnp.exp(d_t[:, :, None] * A) * h + (d_t * u_t)[:, :, None] * B_t[:, None, :]
                y = jnp.einsum('nds,ns->nd', h, C_t)
                return (h, y)
            h0 = jnp.zeros((N, d, s), u.dtype)
            xs = (u.transpose(1, 0, 2), delta.transpose(1, 0, 2), Bm.transpose(1, 0, 2), Cm.transpose(1, 0, 2))
            _, ys = jax.lax.scan(step, h0, xs)
            return ys.transpose(1, 0, 2) + u * Dp

        def mamba(xc, W_in, conv_w, conv_b, W_x, W_dt, b_dt, A_log, Dp, W_out):
            d_inner = W_in.shape[0] // 2
            d_conv = conv_w.shape[-1]
            d_state = A_log.shape[1]
            dt_rank = W_dt.shape[1]
            xz = xc @ W_in.T
            xp, z = jnp.split(xz, 2, axis=-1)
            xt = xp.transpose(0, 2, 1)
            xt = jax.lax.conv_general_dilated(xt, conv_w, window_strides=(1,), padding=[(d_conv - 1, 0)], dimension_numbers=('NCH', 'OIH', 'NCH'), feature_group_count=d_inner)
            xt = jax.nn.silu(xt + conv_b[None, :, None])
            xs = xt.transpose(0, 2, 1)
            dbl = xs @ W_x.T
            dt = dbl[..., :dt_rank]
            Bm = dbl[..., dt_rank:dt_rank + d_state]
            Cm = dbl[..., dt_rank + d_state:]
            delta = jax.nn.softplus(dt @ W_dt.T + b_dt)
            A = -jnp.exp(A_log)
            y = selective_scan(xs, delta, A, Bm, Cm, Dp)
            y = y * jax.nn.silu(z)
            return y @ W_out.T
        key = jax.random.key(seed)
        ks = jax.random.split(key, 10)
        r = lambda k, s, sc=0.02: jax.random.normal(k, s, dtype=jnp.float32) * sc
        return {'x': jax.random.normal(ks[0], (8, INPUT_DIM, 16, 16), dtype=jnp.float32), 'norm_w': jnp.ones((INPUT_DIM,), jnp.float32), 'norm_b': jnp.zeros((INPUT_DIM,), jnp.float32), 'W_in': r(ks[1], (2 * D_INNER, D_MODEL)), 'conv_w': r(ks[2], (D_INNER, 1, D_CONV), 0.1), 'conv_b': jnp.zeros((D_INNER,), jnp.float32), 'W_x': r(ks[3], (DT_RANK + 2 * D_STATE, D_INNER)), 'W_dt': r(ks[4], (D_INNER, DT_RANK), 0.1), 'b_dt': r(ks[5], (D_INNER,), 0.5), 'A_log': jnp.log(jnp.broadcast_to(jnp.arange(1, D_STATE + 1, dtype=jnp.float32), (D_INNER, D_STATE))), 'D': jnp.ones((D_INNER,), jnp.float32), 'W_out': r(ks[6], (D_MODEL, D_INNER)), 'proj_w': r(ks[7], (OUTPUT_DIM, INPUT_DIM)), 'proj_b': jnp.zeros((OUTPUT_DIM,), jnp.float32), 'skip_scale': jnp.ones((1,), jnp.float32)}
    _L1_conv_all = _L1_conv_setup()
    _L1_conv_in = {k: v for k, v in _L1_conv_all.items() if k in ('norm_w', 'norm_b', 'W_in', 'conv_w', 'conv_b', 'W_x', 'W_dt', 'b_dt', 'A_log', 'D', 'W_out', 'proj_w', 'proj_b', 'skip_scale')}
    del _L1_conv_all
    return {'x': x, 'L0_conv_sin': _L0_conv_in['sin'], 'L0_conv_cos': _L0_conv_in['cos'], 'L0_conv_w_qkvo': _L0_conv_in['w_qkvo'], 'L0_conv_b_qkvo': _L0_conv_in['b_qkvo'], 'L0_conv_w_lepe': _L0_conv_in['w_lepe'], 'L0_conv_b_lepe': _L0_conv_in['b_lepe'], 'L0_conv_w_proj': _L0_conv_in['w_proj'], 'L0_conv_b_proj': _L0_conv_in['b_proj'], 'L1_conv_norm_w': _L1_conv_in['norm_w'], 'L1_conv_norm_b': _L1_conv_in['norm_b'], 'L1_conv_W_in': _L1_conv_in['W_in'], 'L1_conv_conv_w': _L1_conv_in['conv_w'], 'L1_conv_conv_b': _L1_conv_in['conv_b'], 'L1_conv_W_x': _L1_conv_in['W_x'], 'L1_conv_W_dt': _L1_conv_in['W_dt'], 'L1_conv_b_dt': _L1_conv_in['b_dt'], 'L1_conv_A_log': _L1_conv_in['A_log'], 'L1_conv_D': _L1_conv_in['D'], 'L1_conv_W_out': _L1_conv_in['W_out'], 'L1_conv_proj_w': _L1_conv_in['proj_w'], 'L1_conv_proj_b': _L1_conv_in['proj_b'], 'L1_conv_skip_scale': _L1_conv_in['skip_scale']}

def reference(x, L0_conv_sin, L0_conv_cos, L0_conv_w_qkvo, L0_conv_b_qkvo, L0_conv_w_lepe, L0_conv_b_lepe, L0_conv_w_proj, L0_conv_b_proj, L1_conv_norm_w, L1_conv_norm_b, L1_conv_W_in, L1_conv_conv_w, L1_conv_conv_b, L1_conv_W_x, L1_conv_W_dt, L1_conv_b_dt, L1_conv_A_log, L1_conv_D, L1_conv_W_out, L1_conv_proj_w, L1_conv_proj_b, L1_conv_skip_scale):
    import jax
    import jax.numpy as jnp

    def _L0_conv_ref(x, sin, cos, w_qkvo, b_qkvo, w_lepe, b_lepe, w_proj, b_proj):
        import jax, jax.numpy as jnp
        import numpy as np
        DIM = 128
        HEADS = 8
        HEAD_DIM = DIM // HEADS
        SCALE = HEAD_DIM ** (-0.5)
        B, H, W = (8, 16, 16)

        def rotate_every_two(x):
            x1 = x[..., ::2]
            x2 = x[..., 1::2]
            return jnp.stack([-x2, x1], axis=-1).reshape(x.shape)

        def theta_shift(x, sin, cos):
            return x * cos + rotate_every_two(x) * sin
        Bx, C, Hx, Wx = x.shape
        N = Hx * Wx
        qkvo = jnp.einsum('bchw,oc->bohw', x, w_qkvo) + b_qkvo[None, :, None, None]
        qkv = qkvo[:, :3 * DIM]
        o = qkvo[:, 3 * DIM:]
        v_sp = qkv[:, 2 * DIM:3 * DIM]
        lepe = jax.lax.conv_general_dilated(v_sp, w_lepe, window_strides=(1, 1), padding=((2, 2), (2, 2)), dimension_numbers=('NCHW', 'OIHW', 'NCHW'), feature_group_count=DIM) + b_lepe[None, :, None, None]
        qkv5 = qkv.reshape(Bx, 3, HEADS, HEAD_DIM, N).transpose(1, 0, 2, 4, 3)
        q, k, v = (qkv5[0], qkv5[1], qkv5[2])
        q = jax.nn.elu(q) + 1.0
        k = jax.nn.elu(k) + 1.0
        q_mean = q.mean(axis=-2, keepdims=True)
        eff = SCALE * jnp.einsum('bnod,bntd->bnot', q_mean, k)
        eff = jax.nn.softmax(eff, axis=-1).swapaxes(-1, -2)
        k = k * eff * N
        q_rope = theta_shift(q, sin, cos)
        k_rope = theta_shift(k, sin, cos)
        z = 1.0 / (jnp.einsum('bntd,bnod->bnto', q, k.mean(axis=-2, keepdims=True)) + 1e-06)
        inv_sqrt_n = N ** (-0.5)
        kv = jnp.einsum('bntd,bnte->bnde', k_rope * inv_sqrt_n, v * inv_sqrt_n)
        res = jnp.einsum('bntd,bnde->bnte', q_rope, kv) * z
        res = res.transpose(0, 1, 3, 2).reshape(Bx, DIM, Hx, Wx)
        res = res + lepe
        out = jnp.einsum('bchw,oc->bohw', res * o, w_proj) + b_proj[None, :, None, None]
        return out

    def _L1_conv_ref(x, norm_w, norm_b, W_in, conv_w, conv_b, W_x, W_dt, b_dt, A_log, D, W_out, proj_w, proj_b, skip_scale):
        import jax, jax.numpy as jnp
        import numpy as np
        INPUT_DIM = 128
        OUTPUT_DIM = 128
        D_STATE = 16
        D_CONV = 4
        EXPAND = 2
        D_MODEL = INPUT_DIM // 4
        D_INNER = EXPAND * D_MODEL
        DT_RANK = (D_MODEL + 15) // 16

        def layernorm(x, w, b, eps=1e-05):
            mu = jnp.mean(x, axis=-1, keepdims=True)
            var = jnp.var(x, axis=-1, keepdims=True)
            return (x - mu) * jax.lax.rsqrt(var + eps) * w + b

        def selective_scan(u, delta, A, Bm, Cm, Dp):
            N, L, d = u.shape
            s = A.shape[1]

            def step(h, inp):
                u_t, d_t, B_t, C_t = inp
                h = jnp.exp(d_t[:, :, None] * A) * h + (d_t * u_t)[:, :, None] * B_t[:, None, :]
                y = jnp.einsum('nds,ns->nd', h, C_t)
                return (h, y)
            h0 = jnp.zeros((N, d, s), u.dtype)
            xs = (u.transpose(1, 0, 2), delta.transpose(1, 0, 2), Bm.transpose(1, 0, 2), Cm.transpose(1, 0, 2))
            _, ys = jax.lax.scan(step, h0, xs)
            return ys.transpose(1, 0, 2) + u * Dp

        def mamba(xc, W_in, conv_w, conv_b, W_x, W_dt, b_dt, A_log, Dp, W_out):
            d_inner = W_in.shape[0] // 2
            d_conv = conv_w.shape[-1]
            d_state = A_log.shape[1]
            dt_rank = W_dt.shape[1]
            xz = xc @ W_in.T
            xp, z = jnp.split(xz, 2, axis=-1)
            xt = xp.transpose(0, 2, 1)
            xt = jax.lax.conv_general_dilated(xt, conv_w, window_strides=(1,), padding=[(d_conv - 1, 0)], dimension_numbers=('NCH', 'OIH', 'NCH'), feature_group_count=d_inner)
            xt = jax.nn.silu(xt + conv_b[None, :, None])
            xs = xt.transpose(0, 2, 1)
            dbl = xs @ W_x.T
            dt = dbl[..., :dt_rank]
            Bm = dbl[..., dt_rank:dt_rank + d_state]
            Cm = dbl[..., dt_rank + d_state:]
            delta = jax.nn.softplus(dt @ W_dt.T + b_dt)
            A = -jnp.exp(A_log)
            y = selective_scan(xs, delta, A, Bm, Cm, Dp)
            y = y * jax.nn.silu(z)
            return y @ W_out.T
        B, C, H, W = x.shape
        L = H * W
        xf = x.reshape(B, C, L).transpose(0, 2, 1)
        xn = layernorm(xf, norm_w, norm_b)
        c4 = C // 4
        ch = jnp.stack(jnp.split(xn, 4, axis=2), axis=0)
        ch = ch.reshape(4 * B, L, c4)
        y = mamba(ch, W_in, conv_w, conv_b, W_x, W_dt, b_dt, A_log, D, W_out)
        y = y + skip_scale * ch
        y = y.reshape(4, B, L, c4).transpose(1, 2, 0, 3).reshape(B, L, C)
        y = layernorm(y, norm_w, norm_b)
        y = y @ proj_w.T + proj_b
        out = y.transpose(0, 2, 1).reshape(B, proj_w.shape[0], H, W)
        return out

    def _gn(v, G=32, eps=1e-05):
        B_, C_, H_, W_ = v.shape
        g = v.reshape(B_, G, C_ // G, H_, W_)
        m = jnp.mean(g, axis=(2, 3, 4), keepdims=True)
        s = jnp.var(g, axis=(2, 3, 4), keepdims=True)
        return ((g - m) / jnp.sqrt(s + eps)).reshape(v.shape)

    def _ln_c(v, eps=1e-06):
        m = jnp.mean(v, axis=1, keepdims=True)
        s = jnp.var(v, axis=1, keepdims=True)
        return (v - m) / jnp.sqrt(s + eps)

    def _ln_t(v, eps=1e-05):
        m = jnp.mean(v, axis=-1, keepdims=True)
        s = jnp.var(v, axis=-1, keepdims=True)
        return (v - m) / jnp.sqrt(s + eps)

    def _to_tokens(v):
        B_, C_, H_, W_ = v.shape
        return v.reshape(B_, C_, H_ * W_).transpose(0, 2, 1)

    def _from_tokens(t, like):
        B_, C_, H_, W_ = like.shape
        return t.transpose(0, 2, 1).reshape(B_, C_, H_, W_)
    x = x + _L0_conv_ref(_gn(x), L0_conv_sin, L0_conv_cos, L0_conv_w_qkvo, L0_conv_b_qkvo, L0_conv_w_lepe, L0_conv_b_lepe, L0_conv_w_proj, L0_conv_b_proj)
    x = x + _L1_conv_ref(_gn(x), L1_conv_norm_w, L1_conv_norm_b, L1_conv_W_in, L1_conv_conv_w, L1_conv_conv_b, L1_conv_W_x, L1_conv_W_dt, L1_conv_b_dt, L1_conv_A_log, L1_conv_D, L1_conv_W_out, L1_conv_proj_w, L1_conv_proj_b, L1_conv_skip_scale)
    return x

_drawn_inputs = setup_inputs


def setup_inputs(seed=0):
    import zlib

    import numpy as np

    out = dict(_drawn_inputs(seed))
    spreads = {'L0_conv_b_qkvo': (0.0, 0.1),
     'L0_conv_b_lepe': (0.0, 0.1),
     'L0_conv_b_proj': (0.0, 0.1),
     'L1_conv_norm_w': (1.0, 0.2),
     'L1_conv_norm_b': (0.0, 0.1),
     'L1_conv_conv_b': (0.0, 0.8),
     'L1_conv_D': (1.0, 0.6),
     'L1_conv_proj_b': (0.0, 0.1)}
    factors = {'L1_conv_W_in': 8.0,
     'L1_conv_conv_w': 8.0,
     'L1_conv_W_x': 8.0,
     'L1_conv_W_dt': 8.0,
     'L1_conv_b_dt': 8.0,
     'L1_conv_A_log': 8.0,
     'L1_conv_W_out': 8.0}
    for name, (base, spread) in spreads.items():
        noise = np.random.default_rng([zlib.crc32(name.encode()), seed]).standard_normal(out[name].shape)
        drawn = base * np.exp(spread * noise) if base else spread * noise
        out[name] = jnp.asarray(drawn.astype(out[name].dtype))
    for name, factor in factors.items():
        out[name] = (out[name] * factor).astype(out[name].dtype)
    return out
```

```python
from contextlib import ExitStack

import concourse.bass as bass
from concourse import mybir

F32 = mybir.dt.float32
BF16 = mybir.dt.bfloat16
ALU = mybir.AluOpType
ACT = mybir.ActivationFunctionType
AX_X = mybir.AxisListType.X

P = 128
B, C, H, W = 8, 128, 16, 16
T = H * W
HEADS, HD = 8, 16
Q, CM = 4, 32
DI, DS, DCONV, DTR = 64, 16, 4, 2
GROUPS, DD = 8, 8
KS, PAD = 5, 2
WP = W + 2 * PAD
GN_EPS = LN_EPS = 1e-5
NPARTS = 3


def columns(widths):
    at, out = 0, {}
    for name, width in widths:
        out[name] = (at, width)
        at += width
    return out, at


W0, W0_COLS = columns([("wqkvo", 4 * C), ("bqkvo", 4), ("wlepe", KS * KS), ("blepe", 1), ("wproj", C),
                       ("bproj", 1), ("cos", T), ("sin", T)])
W1, W1_COLS = columns([("lnw", 1), ("lnb", 1), ("wxp", 2 * P), ("wz", 2 * P), ("convw", DCONV * P), ("convb", 1),
                       ("wB", P), ("wC", P), ("wdt_in", P), ("wdt_out", P), ("bdt", 1), ("alog", GROUPS), ("D", 1),
                       ("wout", 2 * P), ("pw", C), ("pb", 1), ("skip", 1)])
CC, CC_COLS = columns([("ident", P), ("head", P), ("headq", P), ("headk", HEADS), ("rot", P), ("group", P), ("groupsum", P),
                       ("center", P), ("mean", 1), ("selz", 2 * P), ("selr", 2 * P), ("half", P), ("eps", 1),
                       ("pick", 4 * P), ("place", GROUPS * DI)])


def block_kernel(nc, x, w0, w1, cc, out):
    with ExitStack() as ctx:
        def sb(name, shape, dt=F32):
            return ctx.enter_context(nc.sbuf_tensor(name, shape, dt))

        sems = {}

        def S(name):
            if name not in sems:
                sems[name] = ctx.enter_context(nc.semaphore(name))
            return sems[name]

        X = sb("X", [P, B, T])
        W0s, W1s, CCs = sb("W0s", [P, W0_COLS]), sb("W1s", [P, W1_COLS]), sb("CCs", [P, CC_COLS])
        XG = sb("XG", [P, B, T])
        gst, gmv, gin = sb("gst", [P, B, 6]), sb("gmv", [P, B, 2]), sb("gin", [P, B, 2])
        gavg, gnv, gln, grs, gnm = (sb(n, [P, B, w]) for n, w in
                                    (("gavg", 2), ("gnv", 1), ("gln", 1), ("grs", 1), ("gnm", 1)))
        lepe_diag = sb("lepe_diag", [P, KS * KS, P])
        wtap = sb("wtap", [P, 2, DCONV, P])
        wdt = sb("wdt", [P, P])
        negA0, negA = sb("negA0", [P, GROUPS]), sb("negA", [P, GROUPS])
        bout = sb("bout", [P, 1])
        pick = sb("pick", [P, 4, P], BF16)

        e_qk, r_qk = sb("e_qk", [P, 2, T]), sb("r_qk", [P, 2, T])
        QK, kraw = sb("QK", [P, 2, T]), sb("kraw", [P, T])
        qsum, Mq, nmx, Ex, sumE, rE, ksum, Mk = (sb(n, [P, w]) for n, w in (
            ("qsum", 1), ("Mq", P), ("nmx", 1), ("Ex", T), ("sumE", 1), ("rE", 1), ("ksum", 1), ("Mk", HEADS)))
        vS, oS = sb("vS", [P, T]), sb("oS", [P, T])
        vpad = sb("vpad", [P, WP, WP])
        t1, t2, QKR = sb("t1", [P, 2, T]), sb("t2", [P, 2, T]), sb("QKR", [P, 2, T])
        den, zinv, zT, zS = sb("den", [P, 16]), sb("zinv", [P, 16]), sb("zT", [16, P]), sb("zS", [P, T])
        KVT, KVM = sb("KVT", [P, 4, P]), sb("KVM", [P, P])
        u1, u2, u3 = sb("u1", [P, T]), sb("u2", [P, T]), sb("u3", [P, T])
        X1 = [sb(f"X1_{j}", [P, T]) for j in range(2)]
        x1sq, gi, ga, nv, lnv, rs, nm = (sb(n, [P, w]) for n, w in (
            ("x1sq", T), ("gi", 2), ("ga", 2), ("nv", 1), ("lnv", 1), ("rs", 1), ("nm", 1)))
        xg, xc, sq, xl = sb("xg", [P, T]), sb("xc", [P, T]), sb("sq", [P, T]), sb("xl", [P, T])
        lv, r2, rT = sb("lv", [P, 2]), sb("r2", [P, 2]), sb("rT", [2, P])
        XN = [sb(f"XN_{j}", [P, DCONV - 1 + T]) for j in range(2)]
        xs = [sb(f"xs_{j}", [P, 2, T]) for j in range(2)]
        zs = [sb(f"zs_{j}", [P, 2, T]) for j in range(2)]
        ab, rl, em, lnu, um1, cor, dl1 = (sb(n, [P, 2 * T]) for n in ("ab", "rl", "em", "lnu", "um1", "cor", "dl1"))
        Z = sb("Z", [P, 2, 2 * T])
        rem = sb("rem", [P, 2, 2 * T])
        parts = [sb(f"part{i}", [P, 2, 2 * T], BF16) for i in range(NPARTS)]
        R = [sb(f"R_{j}", [NPARTS * 32, 2, 2, 2, 2 * T], BF16) for j in range(2)]
        Bs = [sb(f"Bs_{j}", [P, 2, 2 * T]) for j in range(2)]
        Cs = [sb(f"Cs_{j}", [P, 2, 2 * T]) for j in range(2)]
        dec = [sb(f"dec_{j}", [P, 4, T]) for j in range(2)]
        hst = [sb(f"hst_{j}", [P, 4 * T]) for j in range(2)]
        hc = [sb(f"hc_{j}", [P, 4 * T]) for j in range(2)]
        y1, y2, y3 = sb("y1", [P, 2, T]), sb("y2", [P, 2, T]), sb("y3", [P, T])
        xc2, sq2, lv2, r22, rT2, xl2 = (sb(n, s) for n, s in (
            ("xc2", [P, T]), ("sq2", [P, T]), ("lv2", [P, 2]), ("r22", [P, 2]), ("rT2", [2, P]), ("xl2", [P, T])))
        OUT = [sb(f"OUT_{j}", [P, T]) for j in range(2)]

        F0 = ctx.enter_context(nc.psum_tensor("F0", [P, 512], F32))
        F1 = ctx.enter_context(nc.psum_tensor("F1", [P, 512], F32))
        Y = ctx.enter_context(nc.psum_tensor("Y", [P, 512], F32))
        D = ctx.enter_context(nc.psum_tensor("D", [P, 512], F32))
        DU = [ctx.enter_context(nc.psum_tensor(f"DU_{j}", [P, 2, 512], F32)) for j in range(2)]

        def wt(name, i=0, n=None, rows=P):
            for tile, table in ((W0s, W0), (W1s, W1), (CCs, CC)):
                if name in table:
                    a, w = table[name]
                    n = w if n is None else n
                    return tile[0:rows, a + i:a + i + n]

        x_dram = x.rearrange("b c h w -> c b (h w)")
        out_dram = out.rearrange("b c h w -> c b (h w)")
        block = ctx.enter_context(nc.Block())

        @block.sync
        def _(sp):
            sp.dma_start(X[:], x_dram).then_inc(S("x_loaded"), 16)
            sp.dma_start(CCs[:], cc).then_inc(S("cc_loaded"), 16)
            sp.dma_start(W1s[:], w1).then_inc(S("w1_loaded"), 16)

            def regroup(b, j):
                for i in range(NPARTS):
                    sp.wait_ge(S(f"part{i}_ready"), b + 1)
                    for kg in range(2):
                        for half in range(2):
                            p0 = 64 * half + 32 * kg
                            sp.dma_start(R[j][32 * i:32 * i + 32, kg, :, half, :],
                                         parts[i][p0:p0 + 32, :, :]).then_inc(S("regrouped"), 16)

            with sp.Fori(0, B // 2) as pair:
                for j in range(2):
                    b = 2 * pair + j
                    regroup(b, j)
                    sp.wait_ge(S("f1_read"), b + 2)
                    sp.dma_start(out_dram[:, bass.ds(b, 1), :], OUT[j][:].unsqueeze(1)).then_inc(S("stored"), 16)
            sp.wait_ge(S("stored"), 16 * B)

        @block.tensor
        def _(pe):
            mm = nc.tensor.matmul

            def setup():
                pe.wait_ge(S("cc_loaded"), 16)
                pe.wait_ge(S("w1_loaded"), 16)
                pe.wait_ge(S("gin_ready"), 1)
                mm(F0[:, 0:2 * B], wt("group"), gin[:].rearrange("p b s -> p (b s)"),
                   start=True, stop=True).then_inc(S("gavg_done"), 1)
                mm(F1[:, 0:P], wt("wdt_in", rows=DTR), wt("wdt_out", rows=DTR), start=True, stop=True)
                mm(F1[:, P:P + 1], wt("pw"), wt("lnb"), start=True, stop=True).then_inc(S("wprod_done"), 1)

            def front(b, j):
                pe.wait_ge(S("xg_all"), 1)
                pe.wait_ge(S("f1_read"), b + 1)
                xb = XG[:, bass.ds(b, 1), :]
                pe.wait_ge(S("w0_loaded"), 16)
                for i in range(2):
                    last = mm(F0[:, T * i:T * i + T], wt("wqkvo", C * i, C), xb, start=True, stop=True)
                last.then_inc(S("qk_done"), 1)
                for i in range(2):
                    last = mm(F1[:, T * i:T * i + T], wt("wqkvo", C * (2 + i), C), xb, start=True, stop=True)
                last.then_inc(S("vo_done"), 1)
                yield
                pe.wait_ge(S("k_ready"), b + 1)
                pe.wait_ge(S("mq_ready"), b + 1)
                mm(F0[:, 0:T], Mq[:], kraw[:], start=True, stop=True).then_inc(S("eff_done"), 1)
                yield
                pe.wait_ge(S("vpad_ready"), b + 1)
                pe.wait_ge(S("o_ready"), b + 1)
                for n in range(KS * KS):
                    dy, dx = n // KS, n % KS
                    last = mm(F1[:, 0:T], lepe_diag[:, n, :], vpad[:, dy:dy + H, dx:dx + W],
                              start=(n == 0), stop=(n == KS * KS - 1))
                last.then_inc(S("lepe_done"), 1)
                yield
                pe.wait_ge(S("kk_ready"), b + 1)
                mm(F0[:], wt("rot"), QK[:].rearrange("p a t -> p (a t)"), start=True, stop=True).then_inc(
                    S("rot_done"), 1)
                pe.wait_ge(S("mk_ready"), b + 1)
                pe.wait_ge(S("t2_ready"), b + 1)
                for blk in range(2):
                    last = mm(F0[:, 8 * blk:8 * blk + 8], QK[:, 0, P * blk:P * blk + P], Mk[:], start=True, stop=True)
                last.then_inc(S("den_done"), 1)
                pe.wait_ge(S("zinv_ready"), b + 1)
                nc.tensor.transpose(F0[0:16, P:2 * P], zinv[:], wt("ident")).then_inc(S("zT_done"), 1)
                pe.wait_ge(S("zT_ready"), b + 1)
                for blk in range(2):
                    last = mm(F0[:, 2 * P + P * blk:3 * P + P * blk], wt("selz", P * blk, P, rows=16), zT[:],
                              start=True, stop=True)
                last.then_inc(S("zbc_done"), 1)
                yield
                pe.wait_ge(S("rope_ready"), b + 1)
                pe.wait_ge(S("zS_ready"), b + 1)
                for blk in range(2):
                    nc.tensor.transpose(F0[:, P * blk:P * blk + P], QKR[:, 1, P * blk:P * blk + P], wt("ident"))
                    last = nc.tensor.transpose(F0[:, 2 * P + P * blk:3 * P + P * blk], vS[:, P * blk:P * blk + P],
                                               wt("ident"))
                last.then_inc(S("kvT_done"), 1)
                pe.wait_ge(S("kvT_ready"), b + 1)
                for blk in range(2):
                    last = mm(F0[:, 0:P], KVT[:, blk, :], KVT[:, 2 + blk, :], start=(blk == 0), stop=(blk == 1))
                last.then_inc(S("kv_done"), 1)
                pe.wait_ge(S("kvm_ready"), b + 1)
                mm(F0[:, T:2 * T], KVM[:], QKR[:, 0, :], start=True, stop=True).then_inc(S("res_done"), 1)
                yield
                pe.wait_ge(S("u3_ready"), b + 1)
                mm(F0[:, 0:T], wt("wproj"), u3[:], start=True, stop=True).then_inc(S("proj_done"), 1)
                pe.wait_ge(S("gi_ready"), b + 1)
                mm(F0[:, T:T + 2], wt("groupsum"), gi[:], start=True, stop=True).then_inc(S("g2_done"), 1)
                yield
                pe.wait_ge(S("xg_ready"), b + 1)
                mm(F0[:, 0:T], wt("center"), xg[:], start=True, stop=True).then_inc(S("xc_done"), 1)
                pe.wait_ge(S("sq_ready"), b + 1)
                for blk in range(2):
                    last = mm(F0[:, T + blk:T + blk + 1], sq[:, P * blk:P * blk + P], wt("mean"), start=True, stop=True)
                last.then_inc(S("var_done"), 1)
                pe.wait_ge(S("r2_ready"), b + 1)
                nc.tensor.transpose(F0[0:2, 3 * P:4 * P], r2[:], wt("ident")).then_inc(S("rT_done"), 1)
                pe.wait_ge(S("rT_ready"), b + 1)
                for blk in range(2):
                    last = mm(F0[:, P * blk:P * blk + P], wt("selr", P * blk, P, rows=2), rT[:], start=True, stop=True)
                last.then_inc(S("rbc_done"), 1)
                yield
                pe.wait_ge(S("xn_ready"), b + 1)
                pe.wait_ge(S("u2_ready"), b + 1)
                for qq in range(2):
                    for k in range(DCONV):
                        last = mm(F0[:, T * qq:T * qq + T], wtap[:, qq, k, :], XN[j][:, k:k + T],
                                  start=(k == 0), stop=(k == DCONV - 1))
                last.then_inc(S("xp_done"), 1)
                for qq in range(2):
                    last = mm(F1[:, T * qq:T * qq + T], wt("wz", P * qq, P), XN[j][:, DCONV - 1:], start=True, stop=True)
                last.then_inc(S("z_done"), 1)
                yield
                pe.wait_ge(S("xs_ready"), b + 1)
                xsj = xs[j][:].rearrange("p a t -> p (a t)")
                mm(F0[:], wdt[:], xsj, start=True, stop=True).then_inc(S("dt_done"), 1)
                pe.wait_ge(S("zs_ready"), b + 1)
                for n, (name, half) in enumerate((("wB", 0), ("wB", 1), ("wC", 0), ("wC", 1))):
                    if n == 1:
                        pe.wait_ge(S("abs_ready"), b + 1)
                    if n >= 2:
                        pe.wait_ge(S("bc_read"), 4 * b + n - 1)
                    rows = slice(64 * half, 64 * half + 64)
                    a = W1[name][0]
                    mm((F1, F0)[n % 2][:], W1s[rows, a:a + P], xs[j][rows, :, :].rearrange("p a t -> p (a t)"),
                       start=True, stop=True).then_inc(S("bc_done"), 1)
                yield

            def broadcast(b, j, g):
                u = GROUPS * b + g
                if g == 0:
                    pe.wait_ge(S("regrouped"), 16 * 4 * NPARTS * (b + 1))
                kg, sel = g // 4, pick[0:NPARTS * 32, g % 4, :]
                for half in range(2):
                    if g > 0 or half > 0:
                        pe.wait_ge(S("decay_ready"), 2 * u + half)
                    mm(D[:], sel, R[j][:, kg, 0, half, :], start=True, stop=True).then_inc(S("delta_bc"), 1)
                if g >= 2:
                    pe.wait_ge(S("h_ready"), u - 1)
                for half in range(2):
                    last = mm(DU[g % 2][:, half, :], sel, R[j][:, kg, 1, half, :], start=True, stop=True)
                last.then_inc(S("du_bc"), 1)

            def collect(b, g):
                u = GROUPS * b + g
                pe.wait_ge(S("hc_ready"), u + 1)
                for half in range(2):
                    last = mm(Y[64 * half:64 * half + 64, :], wt("place", DI * g, DI),
                              hc[g % 2][:, 512 * half:512 * half + 512], start=(g == 0), stop=(g == GROUPS - 1))
                last.then_inc(S("y_summed"), 1)

            def back(b, j):
                pe.wait_ge(S("y2_ready"), b + 1)
                for qq in range(2):
                    last = mm(F1[:, 0:T], wt("wout", P * qq, P), y2[:, qq, :], start=(qq == 0), stop=(qq == 1))
                last.then_inc(S("wout_done"), 1)
                pe.wait_ge(S("y3_ready"), b + 1)
                mm(F1[:, 0:T], wt("center"), y3[:], start=True, stop=True).then_inc(S("xc2_done"), 1)
                pe.wait_ge(S("sq2_ready"), b + 1)
                for blk in range(2):
                    last = mm(F1[:, T + blk:T + blk + 1], sq2[:, P * blk:P * blk + P], wt("mean"), start=True, stop=True)
                last.then_inc(S("var2_done"), 1)
                pe.wait_ge(S("r22_ready"), b + 1)
                nc.tensor.transpose(F1[0:2, 3 * P:4 * P], r22[:], wt("ident")).then_inc(S("rT2_done"), 1)
                pe.wait_ge(S("rT2_ready"), b + 1)
                for blk in range(2):
                    last = mm(F1[:, P * blk:P * blk + P], wt("selr", P * blk, P, rows=2), rT2[:], start=True, stop=True)
                last.then_inc(S("rbc2_done"), 1)
                pe.wait_ge(S("xl2_ready"), b + 1)
                mm(F1[:, 0:T], wt("pw"), xl2[:], start=True, stop=True).then_inc(S("proj2_done"), 1)
                yield

            setup()
            with pe.Fori(0, B // 2) as pair:
                for j in range(2):
                    b = 2 * pair + j
                    for _ in front(b, j):
                        pass
                    broadcast(b, j, 0)
                    for g in range(GROUPS):
                        if g + 1 < GROUPS:
                            broadcast(b, j, g + 1)
                        collect(b, g)
                    for _ in back(b, j):
                        pass

        @block.scalar
        def _(act):
            af = nc.scalar.activation
            act.dma_start(W0s[:], w0).then_inc(S("w0_loaded"), 16)

            def setup():
                nc.scalar.preload_act_table_set("natural_log_exp_and_others")
                act.wait_ge(S("w1_loaded"), 16)
                act.wait_ge(S("cc_loaded"), 16)
                af(negA0[:], wt("alog"), ACT.Exp).then_inc(S("expA"), 1)
                act.wait_ge(S("gnv_ready"), 1)
                af(gln[:], gnv[:], ACT.Ln, bias=wt("eps"), scale=-1.0).then_inc(S("gln_ready"), 1)
                act.wait_ge(S("gln_ready"), 1)
                af(grs[:], gln[:], ACT.Exp, scale=-0.5).then_inc(S("grs_ready"), 1)

            def front(b, j):
                act.wait_ge(S("qk_done"), b + 1)
                for i in range(2):
                    bias, src = wt("bqkvo", i, 1), F0[:, T * i:T * i + T]
                    af(e_qk[:, i, :], src, ACT.Exp, bias=bias)
                    af(r_qk[:, i, :], src, ACT.Relu, bias=bias).then_inc(S("qk_act"), 1)
                act.wait_ge(S("vo_done"), b + 1)
                af(vpad[:, PAD:PAD + H, PAD:PAD + W], F1[:, 0:T].rearrange("p (h w) -> p h w", h=H),
                   ACT.Identity, bias=wt("bqkvo", 2, 1)).then_inc(S("vpad_ready"), 1)
                af(vS[:], F1[:, 0:T], ACT.Identity, bias=wt("bqkvo", 2, 1))
                af(oS[:], F1[:, T:2 * T], ACT.Identity, bias=wt("bqkvo", 3, 1)).then_inc(S("o_ready"), 1)
                yield
                act.wait_ge(S("nmx_ready"), b + 1)
                af(Ex[:], F0[:, 0:T], ACT.Exp, bias=nmx[:], accum_out=sumE[:]).then_inc(S("exp_eff"), 1)
                yield
                act.wait_ge(S("zT_done"), b + 1)
                nc.scalar.copy(zT[:], F0[0:16, P:2 * P]).then_inc(S("zT_ready"), 1)
                act.wait_ge(S("zbc_done"), b + 1)
                nc.scalar.copy(zS[:], F0[:, T:2 * T]).then_inc(S("zS_ready"), 1)
                act.wait_ge(S("kvT_done"), b + 1)
                nc.scalar.copy(KVT[:].rearrange("p a t -> p (a t)"), F0[:]).then_inc(S("kvT_ready"), 1)
                yield
                act.wait_ge(S("x1_ready"), b + 1)
                af(x1sq[:], X1[j][:], ACT.Square, accum_out=gi[:, 1:2]).then_inc(S("gi_ready"), 1)
                act.wait_ge(S("nv_ready"), b + 1)
                af(lnv[:], nv[:], ACT.Ln, bias=wt("eps"), scale=-1.0).then_inc(S("lnv_ready"), 1)
                act.wait_ge(S("lnv_ready"), b + 1)
                af(rs[:], lnv[:], ACT.Exp, scale=-0.5).then_inc(S("rs_ready"), 1)
                act.wait_ge(S("xc_done"), b + 1)
                nc.scalar.copy(xc[:], F0[:, 0:T]).then_inc(S("xc_ready"), 1)
                af(sq[:], F0[:, 0:T], ACT.Square).then_inc(S("sq_ready"), 1)
                act.wait_ge(S("var_done"), b + 1)
                af(lv[:], F0[:, T:T + 2], ACT.Ln, bias=wt("eps")).then_inc(S("lv_ready"), 1)
                act.wait_ge(S("lv_ready"), b + 1)
                af(r2[:], lv[:], ACT.Exp, scale=-0.5).then_inc(S("r2_ready"), 1)
                act.wait_ge(S("rT_done"), b + 1)
                nc.scalar.copy(rT[:], F0[0:2, 3 * P:4 * P]).then_inc(S("rT_ready"), 1)
                yield
                act.wait_ge(S("xp_done"), b + 1)
                af(xs[j][:].rearrange("p a t -> p (a t)"), F0[:], ACT.Silu, bias=wt("convb")).then_inc(S("xs_ready"), 1)
                act.wait_ge(S("z_done"), b + 1)
                af(zs[j][:].rearrange("p a t -> p (a t)"), F1[:], ACT.Silu).then_inc(S("zs_ready"), 1)
                nc.scalar.preload_act_table_set("natural_log_exp_and_others")
                yield
                act.wait_ge(S("dt_done"), b + 1)
                af(rl[:], F0[:], ACT.Relu, bias=wt("bdt"))
                af(ab[:], F0[:], ACT.Abs, bias=wt("bdt")).then_inc(S("abs_ready"), 1)
                act.wait_ge(S("abs_ready"), b + 1)
                af(em[:], ab[:], ACT.Exp, scale=-1.0).then_inc(S("em_ready"), 1)
                act.wait_ge(S("em_ready"), b + 1)
                af(lnu[:], em[:], ACT.Ln, bias=1.0).then_inc(S("lnu_ready"), 1)
                for n in range(4):
                    act.wait_ge(S("bc_done"), 4 * b + n + 1)
                    nc.scalar.copy((Bs, Cs)[n // 2][j][:, n % 2, :], (F1, F0)[n % 2][:]).then_inc(S("bc_read"), 1)
                yield
                act.wait_ge(S("z_delta"), b + 1)
                nc.scalar.copy(parts[0][:], Z[:]).then_inc(S("part0_ready"), 1)
                act.wait_ge(S("rem_ready"), b + 1)
                nc.scalar.copy(parts[1][:], rem[:]).then_inc(S("part1_ready"), 1)
                yield

            def decay(b, j, g):
                u = GROUPS * b + g
                if g >= 2:
                    act.wait_ge(S("h_ready"), u - 1)
                for half in range(2):
                    act.wait_ge(S("delta_bc"), 2 * u + half + 1)
                    af(dec[g % 2][:, 2 * half:2 * half + 2, 1:T], D[:].rearrange("p (q t) -> p q t", q=2)[:, :, 1:T],
                       ACT.Exp, scale=negA[:, g:g + 1]).then_inc(S("decay_ready"), 1)

            def back(b, j):
                act.wait_ge(S("xc2_done"), b + 1)
                nc.scalar.copy(xc2[:], F1[:, 0:T]).then_inc(S("xc2_ready"), 1)
                af(sq2[:], F1[:, 0:T], ACT.Square).then_inc(S("sq2_ready"), 1)
                act.wait_ge(S("var2_done"), b + 1)
                af(lv2[:], F1[:, T:T + 2], ACT.Ln, bias=wt("eps")).then_inc(S("lv2_ready"), 1)
                act.wait_ge(S("lv2_ready"), b + 1)
                af(r22[:], lv2[:], ACT.Exp, scale=-0.5).then_inc(S("r22_ready"), 1)
                act.wait_ge(S("rT2_done"), b + 1)
                nc.scalar.copy(rT2[:], F1[0:2, 3 * P:4 * P]).then_inc(S("rT2_ready"), 1)
                yield

            setup()
            act.wait_ge(S("negA_ready"), 1)
            act.wait_ge(S("w0_loaded"), 16)
            act.wait_ge(S("vpad_zero"), 1)
            act.wait_ge(S("borders_zero"), 4)
            with act.Fori(0, B // 2) as pair:
                for j in range(2):
                    b = 2 * pair + j
                    for _ in front(b, j):
                        pass
                    for g in range(GROUPS):
                        decay(b, j, g)
                    for _ in back(b, j):
                        pass

        @block.gpsimd
        def _(pool):
            tt = nc.gpsimd.tensor_tensor
            nc.gpsimd.memset(vpad[:], 0.0).then_inc(S("vpad_zero"), 1)
            for j in range(2):
                nc.gpsimd.memset(XN[j][:, 0:DCONV - 1], 0.0).then_inc(S("borders_zero"), 1)
                nc.gpsimd.memset(dec[j][:, :, 0:1], 0.0).then_inc(S("borders_zero"), 1)
            pool.wait_ge(S("w0_loaded"), 16)

            def front(b, j):
                pool.wait_ge(S("kk_ready"), b + 1)
                tt(t1[:], QK[:], wt("cos").unsqueeze(1).broadcast_to([P, 2, T]), ALU.mult).then_inc(S("t1_ready"), 1)
                pool.wait_ge(S("t1_ready"), b + 1)
                pool.wait_ge(S("t2_ready"), b + 1)
                tt(QKR[:], t1[:], t2[:], ALU.add).then_inc(S("rope_ready"), 1)
                yield
                pool.wait_ge(S("u2_ready"), b + 1)
                tt(u3[:], u2[:], oS[:], ALU.mult).then_inc(S("u3_ready"), 1)
                yield
                pool.wait_ge(S("rem_ready"), b + 1)
                pool.wait_ge(S("part1_ready"), b + 1)
                tt(parts[2][:], rem[:], parts[1][:], ALU.subtract).then_inc(S("part2_ready"), 1)
                yield

            def times_c(b, j, g):
                u = GROUPS * b + g
                pool.wait_ge(S("h_ready"), u + 1)
                if g == 0:
                    pool.wait_ge(S("bc_read"), 4 * b + 4)
                if g >= 2:
                    pool.wait_ge(S("y_summed"), u - 1)
                tt(hc[g % 2][:], hst[g % 2][:], Cs[j][:].rearrange("p a t -> p (a t)"), ALU.mult).then_inc(
                    S("hc_ready"), 1)

            def back(b, j):
                pool.wait_ge(S("y1_ready"), b + 1)
                tt(y2[:], y1[:], zs[j][:], ALU.mult).then_inc(S("y2_ready"), 1)
                yield

            with pool.Fori(0, B // 2) as pair:
                for j in range(2):
                    b = 2 * pair + j
                    for _ in front(b, j):
                        pass
                    for g in range(GROUPS):
                        times_c(b, j, g)
                    for _ in back(b, j):
                        pass

        @block.vector
        def _(dve):
            v = nc.vector

            def setup():
                dve.wait_ge(S("x_loaded"), 16)
                for b in range(B):
                    v.bn_stats(gst[:, b, :], X[:, b, :]).then_inc(S("gst_ready"), 1)
                for b in range(B):
                    dve.wait_ge(S("gst_ready"), b + 1)
                    v.bn_aggr(gmv[:, b, :], gst[:, b, :]).then_inc(S("gmv_ready"), 1)
                dve.wait_ge(S("gmv_ready"), B)
                v.tensor_tensor(gnm[:], gmv[:, :, 0:1], gmv[:, :, 0:1], ALU.mult).then_inc(S("gsq_ready"), 1)
                v.tensor_copy(gin[:, :, 0:1], gmv[:, :, 0:1])
                dve.wait_ge(S("gsq_ready"), 1)
                v.tensor_tensor(gin[:, :, 1:2], gnm[:], gmv[:, :, 1:2], ALU.add).then_inc(S("gin_ready"), 1)
                dve.wait_ge(S("gavg_done"), 1)
                v.tensor_copy(gavg[:].rearrange("p b s -> p (b s)"), F0[:, 0:2 * B]).then_inc(S("gavg_ready"), 1)
                dve.wait_ge(S("gavg_ready"), 1)
                v.tensor_tensor(gnm[:], gavg[:, :, 0:1], gavg[:, :, 0:1], ALU.mult).then_inc(S("gsq_ready"), 1)
                dve.wait_ge(S("gsq_ready"), 2)
                v.tensor_tensor(gnv[:], gnm[:], gavg[:, :, 1:2], ALU.subtract).then_inc(S("gnv_ready"), 1)
                dve.wait_ge(S("grs_ready"), 1)
                v.scalar_tensor_tensor(out=gnm[:], in0=gavg[:, :, 0:1], scalar=-1.0, in1=grs[:], op0=ALU.mult,
                                       op1=ALU.mult).then_inc(S("gnm_ready"), 1)
                dve.wait_ge(S("gnm_ready"), 1)
                for b in range(B):
                    last = v.tensor_scalar(XG[:, b, :], X[:, b, :], grs[:, b, :], gnm[:, b, :], ALU.mult, ALU.add)
                last.then_inc(S("xg_all"), 1)
                dve.wait_ge(S("w0_loaded"), 16)
                dve.wait_ge(S("w1_loaded"), 16)
                dve.wait_ge(S("wprod_done"), 1)
                v.tensor_tensor(wdt[:], F1[:, 0:P], wt("half"), ALU.mult)
                v.tensor_tensor(bout[:], F1[:, P:P + 1], wt("pb"), ALU.add).then_inc(S("f1_read"), 1)
                for n in range(KS * KS):
                    v.tensor_scalar(lepe_diag[:, n, :], wt("ident"), wt("wlepe", n, 1), None, ALU.mult)
                for qq in range(2):
                    v.tensor_tensor(wtap[:, qq, :, :],
                                    wt("wxp", P * qq, P).unsqueeze(1).broadcast_to([P, DCONV, P]),
                                    wt("convw").rearrange("p (k m) -> p k m", k=DCONV), ALU.mult)
                v.tensor_copy(pick[:].rearrange("p a m -> p (a m)"), wt("pick"))
                dve.wait_ge(S("expA"), 1)
                v.tensor_scalar(negA[:], negA0[:], -1.0, None, ALU.mult).then_inc(S("negA_ready"), 1)

            def front(b, j):
                dve.wait_ge(S("qk_act"), 2 * b + 1)
                v.scalar_tensor_tensor(out=QK[:, 0, :], in0=e_qk[:, 0, :], scalar=1.0, in1=r_qk[:, 0, :],
                                       op0=ALU.min, op1=ALU.add, accum_out=qsum[:]).then_inc(S("q_ready"), 1)
                dve.wait_ge(S("q_ready"), b + 1)
                v.tensor_scalar(Mq[:], wt("headq"), qsum[:], None, ALU.mult).then_inc(S("mq_ready"), 1)
                dve.wait_ge(S("qk_act"), 2 * b + 2)
                v.scalar_tensor_tensor(out=kraw[:], in0=e_qk[:, 1, :], scalar=1.0, in1=r_qk[:, 1, :],
                                       op0=ALU.min, op1=ALU.add).then_inc(S("k_ready"), 1)
                yield
                dve.wait_ge(S("eff_done"), b + 1)
                v.tensor_reduce(nmx[:], F0[:, 0:T], AX_X, ALU.max, negate=True).then_inc(S("nmx_ready"), 1)
                yield
                dve.wait_ge(S("exp_eff"), b + 1)
                v.reciprocal(rE[:], sumE[:]).then_inc(S("rE_ready"), 1)
                dve.wait_ge(S("rE_ready"), b + 1)
                dve.wait_ge(S("k_ready"), b + 1)
                v.scalar_tensor_tensor(out=QK[:, 1, :], in0=Ex[:], scalar=rE[:], in1=kraw[:],
                                       op0=ALU.mult, op1=ALU.mult, accum_out=ksum[:]).then_inc(S("kk_ready"), 1)
                dve.wait_ge(S("kk_ready"), b + 1)
                v.tensor_scalar(Mk[:], wt("headk"), ksum[:], None, ALU.mult).then_inc(S("mk_ready"), 1)
                yield
                dve.wait_ge(S("rot_done"), b + 1)
                v.tensor_tensor(t2[:], F0[:].rearrange("p (a t) -> p a t", a=2),
                                wt("sin").unsqueeze(1).broadcast_to([P, 2, T]), ALU.mult).then_inc(S("t2_ready"), 1)
                dve.wait_ge(S("den_done"), b + 1)
                v.tensor_scalar(den[:], F0[:, 0:16], 1e-6, None, ALU.add).then_inc(S("den_ready"), 1)
                dve.wait_ge(S("den_ready"), b + 1)
                v.reciprocal(zinv[:], den[:]).then_inc(S("zinv_ready"), 1)
                yield
                dve.wait_ge(S("kv_done"), b + 1)
                v.tensor_tensor(KVM[:], F0[:, 0:P], wt("head"), ALU.mult).then_inc(S("kvm_ready"), 1)
                dve.wait_ge(S("res_done"), b + 1)
                dve.wait_ge(S("zS_ready"), b + 1)
                v.tensor_tensor(u1[:], F0[:, T:2 * T], zS[:], ALU.mult).then_inc(S("u1_ready"), 1)
                dve.wait_ge(S("lepe_done"), b + 1)
                dve.wait_ge(S("u1_ready"), b + 1)
                v.scalar_tensor_tensor(out=u2[:], in0=F1[:, 0:T], scalar=wt("blepe"), in1=u1[:],
                                       op0=ALU.add, op1=ALU.add).then_inc(S("u2_ready"), 1)
                yield
                dve.wait_ge(S("proj_done"), b + 1)
                v.scalar_tensor_tensor(out=X1[j][:].unsqueeze(1), in0=F0[:, 0:T].unsqueeze(1), scalar=wt("bproj"),
                                       in1=X[:, bass.ds(b, 1), :], op0=ALU.add, op1=ALU.add,
                                       accum_out=gi[:, 0:1]).then_inc(S("x1_ready"), 1)
                yield
                dve.wait_ge(S("g2_done"), b + 1)
                v.tensor_copy(ga[:], F0[:, T:T + 2]).then_inc(S("ga_ready"), 1)
                dve.wait_ge(S("ga_ready"), b + 1)
                v.scalar_tensor_tensor(out=nv[:], in0=ga[:, 0:1], scalar=ga[:, 0:1], in1=ga[:, 1:2],
                                       op0=ALU.mult, op1=ALU.subtract).then_inc(S("nv_ready"), 1)
                dve.wait_ge(S("rs_ready"), b + 1)
                v.tensor_scalar(nm[:], ga[:, 0:1], rs[:], -1.0, ALU.mult, ALU.mult).then_inc(S("nm_ready"), 1)
                dve.wait_ge(S("nm_ready"), b + 1)
                v.tensor_scalar(xg[:], X1[j][:], rs[:], nm[:], ALU.mult, ALU.add).then_inc(S("xg_ready"), 1)
                yield
                dve.wait_ge(S("rbc_done"), b + 1)
                dve.wait_ge(S("xc_ready"), b + 1)
                v.scalar_tensor_tensor(out=xl[:], in0=xc[:], scalar=wt("lnw"), in1=F0[:, 0:T],
                                       op0=ALU.mult, op1=ALU.mult).then_inc(S("xl_ready"), 1)
                dve.wait_ge(S("xl_ready"), b + 1)
                v.tensor_scalar(XN[j][:, DCONV - 1:], xl[:], wt("lnb"), None, ALU.add).then_inc(S("xn_ready"), 1)
                yield
                dve.wait_ge(S("em_ready"), b + 1)
                v.tensor_scalar(um1[:], em[:], 1.0, None, ALU.add).then_inc(S("um1_ready"), 1)
                dve.wait_ge(S("um1_ready"), b + 1)
                v.scalar_tensor_tensor(out=cor[:], in0=um1[:], scalar=1.0, in1=em[:],
                                       op0=ALU.subtract, op1=ALU.subtract).then_inc(S("cor_ready"), 1)
                dve.wait_ge(S("cor_ready"), b + 1)
                dve.wait_ge(S("lnu_ready"), b + 1)
                v.tensor_tensor(dl1[:], lnu[:], cor[:], ALU.subtract).then_inc(S("dl1_ready"), 1)
                dve.wait_ge(S("dl1_ready"), b + 1)
                v.tensor_tensor(Z[:, 0, :], dl1[:], rl[:], ALU.add).then_inc(S("delta_ready"), 1)
                dve.wait_ge(S("delta_ready"), b + 1)
                v.tensor_tensor(Z[:, 1, :], Z[:, 0, :], xs[j][:].rearrange("p a t -> p (a t)"), ALU.mult).then_inc(
                    S("z_delta"), 1)
                dve.wait_ge(S("z_delta"), b + 1)
                dve.wait_ge(S("part0_ready"), b + 1)
                v.tensor_tensor(rem[:], Z[:], parts[0][:], ALU.subtract).then_inc(S("rem_ready"), 1)
                yield

            def recur(b, j, g):
                u = GROUPS * b + g
                du = DU[g % 2][:].rearrange("p a t -> p (a t)")
                dve.wait_ge(S("du_bc"), u + 1)
                if g == 0:
                    dve.wait_ge(S("bc_read"), 4 * b + 2)
                v.tensor_tensor(du, du, Bs[j][:].rearrange("p a t -> p (a t)"), ALU.mult).then_inc(S("b_ready"), 1)
                dve.wait_ge(S("b_ready"), u + 1)
                dve.wait_ge(S("decay_ready"), 2 * u + 2)
                if g >= 2:
                    dve.wait_ge(S("hc_ready"), u - 1)
                v.tensor_tensor_scan(hst[g % 2][:], dec[g % 2][:].rearrange("p a t -> p (a t)"), du, 0.0,
                                     ALU.mult, ALU.add).then_inc(S("h_ready"), 1)

            def back(b, j):
                dve.wait_ge(S("y_summed"), GROUPS * (b + 1))
                v.scalar_tensor_tensor(out=y1[:].rearrange("p a t -> p (a t)"),
                                       in0=xs[j][:].rearrange("p a t -> p (a t)"), scalar=wt("D"), in1=Y[:],
                                       op0=ALU.mult, op1=ALU.add).then_inc(S("y1_ready"), 1)
                dve.wait_ge(S("wout_done"), b + 1)
                v.scalar_tensor_tensor(out=y3[:], in0=XN[j][:, DCONV - 1:], scalar=wt("skip"), in1=F1[:, 0:T],
                                       op0=ALU.mult, op1=ALU.add).then_inc(S("y3_ready"), 1)
                dve.wait_ge(S("rbc2_done"), b + 1)
                dve.wait_ge(S("xc2_ready"), b + 1)
                v.scalar_tensor_tensor(out=xl2[:], in0=xc2[:], scalar=wt("lnw"), in1=F1[:, 0:T],
                                       op0=ALU.mult, op1=ALU.mult).then_inc(S("xl2_ready"), 1)
                dve.wait_ge(S("proj2_done"), b + 1)
                v.scalar_tensor_tensor(out=OUT[j][:], in0=F1[:, 0:T], scalar=bout[:], in1=X1[j][:],
                                       op0=ALU.add, op1=ALU.add).then_inc(S("f1_read"), 1)
                yield

            setup()
            dve.wait_ge(S("borders_zero"), 4)
            with dve.Fori(0, B // 2) as pair:
                for j in range(2):
                    b = 2 * pair + j
                    for _ in front(b, j):
                        pass
                    for g in range(GROUPS):
                        recur(b, j, g)
                    for _ in back(b, j):
                        pass


def kernel(**inputs):
    import numpy as np
    import concourse.bacc as bacc
    from concourse.bass_utils import run_bass_kernel_spmd as run

    a = {k: np.asarray(v) for k, v in inputs.items()}
    f = np.float32

    def pack(table, cols, named):
        out = np.zeros((P, cols), f)
        for name, block in named.items():
            start, width = table[name]
            out[:block.shape[0], start:start + width] = block.reshape(block.shape[0], width)
        return out

    def col(v):
        return v.reshape(-1, 1)

    w0 = pack(W0, W0_COLS, {
        "wqkvo": a["L0_conv_w_qkvo"].T, "bqkvo": a["L0_conv_b_qkvo"].reshape(4, C).T,
        "wlepe": a["L0_conv_w_lepe"].reshape(C, KS * KS), "blepe": col(a["L0_conv_b_lepe"]),
        "wproj": a["L0_conv_w_proj"].T, "bproj": col(a["L0_conv_b_proj"]),
        "cos": np.tile(a["L0_conv_cos"].T, (HEADS, 1)), "sin": np.tile(a["L0_conv_sin"].T, (HEADS, 1))})

    W_in, W_x, W_out = a["L1_conv_W_in"], a["L1_conv_W_x"], a["L1_conv_W_out"]
    wxp, wz, wout = (np.zeros((P, 2, P), f) for _ in range(3))
    for qq in range(2):
        for half in range(2):
            c, m = slice(CM * (2 * qq + half), CM * (2 * qq + half) + CM), slice(DI * half, DI * half + DI)
            wxp[c, qq, m] = W_in[:DI].T
            wz[c, qq, m] = W_in[DI:].T
            wout[m, qq, c] = W_out.T
    both = lambda v: np.concatenate([v, v], 0)
    w1 = pack(W1, W1_COLS, {
        "lnw": col(a["L1_conv_norm_w"]), "lnb": col(a["L1_conv_norm_b"]), "wxp": wxp, "wz": wz,
        "convw": np.broadcast_to(both(a["L1_conv_conv_w"][:, 0, :]).T[None], (P, DCONV, P)),
        "convb": col(both(a["L1_conv_conv_b"])),
        "wB": both(np.tile(W_x[DTR:DTR + DS].T, (1, DD))), "wC": both(np.tile(W_x[DTR + DS:].T, (1, DD))),
        "wdt_in": both(W_x[:DTR].T).T, "wdt_out": both(a["L1_conv_W_dt"]).T, "bdt": col(both(a["L1_conv_b_dt"])),
        "alog": a["L1_conv_A_log"].reshape(GROUPS, DD * DS).T, "D": col(both(a["L1_conv_D"])), "wout": wout,
        "pw": a["L1_conv_proj_w"].T, "pb": col(a["L1_conv_proj_b"]),
        "skip": np.broadcast_to(a["L1_conv_skip_scale"].reshape(1, 1), (P, 1))})

    c = np.arange(P)
    ident = np.eye(P, dtype=f)
    head = (c[:, None] // HD == c[None] // HD).astype(f)
    rot = np.zeros((P, P), f)
    rot[c[1::2], c[0::2]] = -1
    rot[c[0::2], c[1::2]] = 1
    selz, selr = np.zeros((16, 2, P), f), np.zeros((2, 2, P), f)
    for blk in range(2):
        selz[8 * blk + c // HD, blk, c] = 1
        selr[blk, blk, :] = 1
    pick = np.zeros((NPARTS, 32, 4, P), f)
    place = np.zeros((P, GROUPS, DI), f)
    for g in range(GROUPS):
        place[c, g, DD * g + c // DS] = 1
    for s in range(4):
        pick[:, DD * s + c // DS, s, c] = 1
    cc = pack(CC, CC_COLS, {
        "ident": ident, "head": head, "headq": head * f(HD ** -0.5 / T), "headk": head[:, ::HD], "rot": rot,
        "group": (c[:, None] // 4 == c[None] // 4).astype(f) / 4,
        "groupsum": (c[:, None] // 4 == c[None] // 4).astype(f) / (4 * T), "center": ident - f(1 / C),
        "mean": np.full((P, 1), 1 / C, f), "selz": selz, "selr": selr,
        "half": (c[:, None] // DI == c[None] // DI).astype(f), "eps": np.full((P, 1), LN_EPS, f),
        "pick": pick.reshape(NPARTS * 32, 4 * P), "place": place})

    nc = bacc.Bacc("TRN2", target_bir_lowering=False, num_devices=1)
    arrays, args = {}, []
    for name, v in (("x", a["x"]), ("w0", w0), ("w1", w1), ("cc", cc)):
        arrays[name] = np.ascontiguousarray(v)
        args.append(nc.dram_tensor(name, v.shape, mybir.dt.from_np(v.dtype), kind="ExternalInput").ap())
    out = nc.dram_tensor("out", (B, C, H, W), F32, kind="ExternalOutput").ap()
    block_kernel(nc, *args, out)
    r = run(nc, [arrays], core_ids=[0])
    return r.results[0]["out"]
```

```python
from contextlib import ExitStack

import concourse.bass as bass
from concourse import mybir

F32 = mybir.dt.float32
BF16 = mybir.dt.bfloat16
ALU = mybir.AluOpType
ACT = mybir.ActivationFunctionType
AX_X = mybir.AxisListType.X

P = 128
B, C, H, W = 8, 128, 16, 16
T = H * W
HEADS, HD = 8, 16
Q, CM = 4, 32
DI, DS, DCONV, DTR = 64, 16, 4, 2
GROUPS, DD = 8, 8
KS, PAD = 5, 2
WP = W + 2 * PAD
ROUNDS = 9
SHIFTS = (0, 1, WP, WP + 1)
GN_EPS = LN_EPS = 1e-5
NPARTS = 3


def columns(widths):
    at, out = 0, {}
    for name, width in widths:
        out[name] = (at, width)
        at += width
    return out, at


W0, W0_COLS = columns([("wqkvo", 4 * C), ("bqkvo", 4), ("wlepe", Q * ROUNDS), ("blepe", 1), ("wproj", C),
                       ("bproj", 1), ("cos", T), ("sin", T)])
W1, W1_COLS = columns([("lnw", 1), ("lnb", 1), ("wxp", DI), ("wz", DI), ("convw", DI), ("convb", 1),
                       ("wBC", 2 * 2 * DS), ("wdt_in", P), ("wdt_out", P), ("bdt", 1), ("alog", GROUPS), ("D", 1),
                       ("wout", 2 * P), ("pw", C), ("pb", 1), ("skip", 1)])
CC, CC_COLS = columns([("group", P), ("ident", P), ("head", P), ("headq", P), ("rot", P), ("groupsum", P),
                       ("center", P), ("mean", P), ("half", P), ("eps", 1), ("zeps", 1),
                       ("pick", 4 * P), ("place", GROUPS * DI), ("ident32", CM)])


def block_kernel(nc, x, w0, w1, cc, out):
    with ExitStack() as ctx:
        def sb(name, shape, dt=F32):
            return ctx.enter_context(nc.sbuf_tensor(name, shape, dt))

        sems = {}

        def S(name):
            if name not in sems:
                sems[name] = ctx.enter_context(nc.semaphore(name))
            return sems[name]

        X = sb("X", [P, B, T])
        W0s, W1s, CCs = sb("W0s", [P, W0_COLS]), sb("W1s", [P, W1_COLS]), sb("CCs", [P, CC_COLS])
        gst, gmv, gin = sb("gst", [P, B, 6]), sb("gmv", [P, B, 2]), sb("gin", [P, B, 2])
        gavg, gnv, gln, grs, gnm = (sb(n, [P, B, w]) for n, w in
                                    (("gavg", 2), ("gnv", 1), ("gln", 1), ("grs", 1), ("gnm", 1)))
        wpatch = sb("wpatch", [P, Q * ROUNDS, CM])
        wtap = sb("wtap", [P, DI])
        wdt = sb("wdt", [P, P])
        negA0, negA = sb("negA0", [P, GROUPS]), sb("negA", [P, GROUPS])
        bout = sb("bout", [P, 1])
        pick = sb("pick", [P, 4, P], BF16)

        xg0, e_qk, r_qk = sb("xg0", [P, T]), sb("e_qk", [P, 2, T]), sb("r_qk", [P, 2, T])
        QK, kraw = sb("QK", [P, 2, T]), sb("kraw", [P, T])
        qsum, Mq, nmx, Ex, sumE, rE, ksum, Mk = (sb(n, [P, w]) for n, w in (
            ("qsum", 1), ("Mq", P), ("nmx", 1), ("Ex", T), ("sumE", 1), ("rE", 1), ("ksum", 1), ("Mk", P)))
        vS, oS = sb("vS", [P, T]), [sb(f"oS_{j}", [P, T]) for j in range(2)]
        vpad = sb("vpad", [P, WP * WP + SHIFTS[-1]])
        V4 = sb("V4", [P, Q, WP * WP])
        t1, t2 = sb("t1", [P, 2, T]), sb("t2", [P, 2, T])
        QKR = [sb(f"QKR_{j}", [P, 2, T]) for j in range(2)]
        lz, zS = sb("lz", [P, T]), [sb(f"zS_{j}", [P, T]) for j in range(2)]
        KVT, KVM = sb("KVT", [P, 4, P]), [sb(f"KVM_{j}", [P, P]) for j in range(2)]
        u1, u2, u3 = sb("u1", [P, T]), sb("u2", [P, T]), sb("u3", [P, T])
        x1sq, gi, ga, nv, lnv, rs, nm = (sb(n, [P, w]) for n, w in (
            ("x1sq", T), ("gi", 2), ("ga", 2), ("nv", 1), ("lnv", 1), ("rs", 1), ("nm", 1)))
        xg, sq, lr, rr, xl = (sb(n, [P, T]) for n in ("xg", "sq", "lr", "rr", "xl"))
        XN = [sb(f"XN_{j}", [P, DCONV - 1 + T]) for j in range(2)]
        XN4 = sb("XN4", [P, Q, T])
        xk = [sb(f"xk_{j}", [P, T]) for j in range(2)]
        xs = [sb(f"xs_{j}", [P, 2, T]) for j in range(2)]
        zs = [sb(f"zs_{j}", [P, 2, T]) for j in range(2)]
        ab, rl, em, lnu, um1, cor, dl1 = (sb(n, [P, 2 * T]) for n in ("ab", "rl", "em", "lnu", "um1", "cor", "dl1"))
        Z = sb("Z", [P, 2, 2 * T])
        parts = [sb(f"part{i}", [P, 2, 2 * T], BF16) for i in range(NPARTS)]
        R = [sb(f"R_{j}", [NPARTS * 32, 2, 2, 2, 2 * T], BF16) for j in range(2)]
        bc = sb("bc", [2 * 2 * DS, 2 * T])
        Bs = [sb(f"Bs_{j}", [P, 2, 2 * T]) for j in range(2)]
        Cs = [sb(f"Cs_{j}", [P, 2, 2 * T]) for j in range(2)]
        dec = [sb(f"dec_{j}", [P, 4, T]) for j in range(4)]
        bin_ = [sb(f"bin_{j}", [P, 4 * T]) for j in range(2)]
        hst = [sb(f"hst_{j}", [P, 4 * T]) for j in range(4)]
        y1, y2, y3 = sb("y1", [P, 2, T]), sb("y2", [P, 2, T]), sb("y3", [P, T])
        sq2, lr2, rr2, xl2 = (sb(n, [P, T]) for n in ("sq2", "lr2", "rr2", "xl2"))

        F0, F1, F2, F3, Y, D = (ctx.enter_context(nc.psum_tensor(n, [P, 512], F32))
                                for n in ("F0", "F1", "F2", "F3", "Y", "D"))
        DU = ctx.enter_context(nc.psum_tensor("DU", [P, 2, 512], F32))

        def flat(ap):
            return ap.rearrange("p a t -> p (a t)")

        def wt(name, i=0, n=None, rows=P):
            for tile, table in ((W0s, W0), (W1s, W1), (CCs, CC)):
                if name in table:
                    a, w = table[name]
                    n = w if n is None else n
                    return tile[0:rows, a + i:a + i + n]

        def wait(eng, name, count):
            if not isinstance(count, int) or count > 0:
                eng.wait_ge(S(name), count)

        def segment(works, s):
            for work in works:
                while work[1] == s:
                    work[1] = next(work[0], None)

        def periods(eng, chains, start, unit, finish, weights=lambda: None):
            def works(*batches):
                begun = [chain(b, j) for chain, (b, j) in zip(chains[::-1], batches[::-1]) if b is not None]
                return [[steps, next(steps, None)] for steps in begun]

            def run(*batches):
                w = works(*batches)
                for s in range(SEGMENTS):
                    segment(w, s)

            def period(b, j, ahead=3, behind=True):
                none = (None, 0)
                w = works((b + 3, 1 - j) if ahead > 2 else none, (b + 2, j) if ahead > 1 else none,
                          (b + 1, 1 - j) if ahead > 0 else none, (b - 1, 1 - j) if behind else none)
                for g in range(GROUPS):
                    seg = iter((2 * g, 2 * g + 1))
                    unit(b, j, g, lambda: segment(w, next(seg)), ahead > 0)

            none = (None, 0)
            run((0, 0), none, none, none)
            weights()
            run((1, 1), (0, 0), none, none)
            run((2, 0), (1, 1), (0, 0), none)
            start()
            period(0, 0, behind=False)
            with eng.Fori(0, (B - 4) // 2) as pair:
                period(2 * pair + 1, 1)
                period(2 * pair + 2, 0)
            for left in (2, 1, 0):
                period(B - 1 - left, (B - 1 - left) % 2, ahead=left)
            finish()
            run(none, none, none, (B - 1, 1))

        SEGMENTS = 2 * GROUPS
        LAG = 1
        LEAD = 2
        v_dram = nc.dram_tensor("v_scratch", [P, WP * WP + SHIFTS[-1]], F32).ap()
        xn_dram = nc.dram_tensor("xn_scratch", [P, DCONV - 1 + T], F32).ap()
        bc_dram = nc.dram_tensor("bc_scratch", [2, DS, 2 * 2 * T], F32).ap()
        x_dram = x.rearrange("b c h w -> c b (h w)")
        out_dram = out.rearrange("b c h w -> c b (h w)")
        block = ctx.enter_context(nc.Block())

        @block.sync
        def _(sp):
            sp.dma_start(X[:, 0:B // 2, :], x_dram[:, 0:B // 2, :]).then_inc(S("x_loaded"), 16)
            sp.dma_start(CCs[:, 0:P], cc[:, 0:P]).then_inc(S("group_loaded"), 16)
            sp.dma_start(CCs[:, P:], cc[:, P:]).then_inc(S("cc_loaded"), 16)
            sp.dma_start(W1s[:], w1).then_inc(S("w1_loaded"), 16)

            def front(b, j):
                yield 12
                sp.wait_ge(S("vpad_ready"), b + 1)
                sp.dma_start(v_dram, vpad[:]).then_inc(S("v_out"), 16)
                yield 14
                sp.wait_ge(S("v_out"), 16 * (b + 1))
                for n, off in enumerate(SHIFTS):
                    sp.dma_start(V4[CM * n:CM * n + CM, :, :],
                                 v_dram[:, off:off + WP * WP].rearrange("(q c) n -> c q n", q=Q)).then_inc(
                                     S("v_shifted"), 16)

            def mid(b, j):
                yield 12
                sp.wait_ge(S("xn_ready"), b + 1)
                sp.dma_start(xn_dram, XN[j][:]).then_inc(S("xn_out"), 16)
                yield 13
                sp.wait_ge(S("xn_out"), 16 * (b + 1))
                for k in range(DCONV):
                    sp.dma_start(XN4[CM * k:CM * k + CM, :, :],
                                 xn_dram[:, k:k + T].rearrange("(q c) t -> c q t", q=Q)).then_inc(S("xn_shifted"), 16)

            def tail(b, j):
                yield 4
                sp.wait_ge(S("bc_ready"), b + 1)
                sp.dma_start(bc_dram.rearrange("w s (h n) -> h (w s) n", h=2), bc[:]).then_inc(S("bc_out"), 16)
                yield 4
                sp.wait_ge(S("bc_out"), 16 * (b + 1))
                for which, copies in enumerate((Bs[j], Cs[j])):
                    sp.dma_start(flat(copies[:]), bc_dram[which].unsqueeze(0).broadcast_to(
                        [DD, DS, 2 * 2 * T])).then_inc(S("bc_copied"), 16)
                for i in range(NPARTS):
                    yield (4, 10, 12)[i]
                    sp.wait_ge(S(f"part{i}_ready"), b + 1)
                    for half in range(2):
                        for kg in range(2):
                            p0 = 64 * half + 32 * kg
                            sp.dma_start(R[j][32 * i:32 * i + 32, kg, :, half, :],
                                         parts[i][p0:p0 + 32, :, :]).then_inc(S("regrouped"), 16)

            def back(b, j):
                yield 15
                sp.wait_ge(S("f3_read"), b + 2)
                sp.dma_start(out_dram[:, bass.ds(b, 1), :], X[:, bass.ds(b, 1), :]).then_inc(S("stored"), 16)

            def unit(b, j, g, side, more):
                side()
                side()

            periods(sp, (front, mid, tail, back), lambda: None, unit, lambda: None)
            sp.wait_ge(S("stored"), 16 * B)

        @block.tensor
        def _(pe):
            mm = nc.tensor.matmul

            def setup():
                pe.wait_ge(S("group_loaded"), 16)
                pe.wait_ge(S("gin_ready"), 1)
                mm(F0[:, 0:2 * B], wt("group"), gin[:].rearrange("p b s -> p (b s)"),
                   start=True, stop=True).then_inc(S("gavg_done"), 1)
                pe.wait_ge(S("cc_loaded"), 16)
                pe.wait_ge(S("w0_loaded"), 16)

            def weights():
                pe.wait_ge(S("w1_loaded"), 16)
                mm(F3[:, 0:P], wt("wdt_in", rows=DTR), wt("wdt_out", rows=DTR), start=True, stop=True)
                mm(F3[:, P:P + 1], wt("pw"), wt("lnb"), start=True, stop=True).then_inc(S("wprod_done"), 1)
                pe.wait_ge(S("weights_ready"), 1)

            def front(b, j):
                yield 1
                pe.wait_ge(S("xg0_ready"), b + 1)
                wait(pe, "kvm_ready", b)
                for i in range(2):
                    last = mm(F0[:, T * i:T * i + T], wt("wqkvo", C * i, C), xg0[:], start=True, stop=True)
                last.then_inc(S("qk_done"), 1)
                yield 5
                pe.wait_ge(S("qk_act"), 2 * b + 2)
                for i in range(2):
                    last = mm(F0[:, T * i:T * i + T], wt("wqkvo", C * (2 + i), C), xg0[:], start=True, stop=True)
                last.then_inc(S("vo_done"), 1)
                yield 7
                pe.wait_ge(S("k_ready"), b + 1)
                pe.wait_ge(S("mq_ready"), b + 1)
                pe.wait_ge(S("o_ready"), b + 1)
                mm(F0[:, 0:T], Mq[:], kraw[:], start=True, stop=True).then_inc(S("eff_done"), 1)
                yield 10
                pe.wait_ge(S("kk_ready"), b + 1)
                mm(F0[:], wt("rot"), flat(QK[:]), start=True, stop=True).then_inc(S("rot_done"), 1)
                yield 12
                pe.wait_ge(S("mk_ready"), b + 1)
                pe.wait_ge(S("t2_ready"), b + 1)
                mm(F0[:, 0:T], Mk[:], QK[:, 0, :], start=True, stop=True).then_inc(S("den_done"), 1)
                yield 13
                pe.wait_ge(S("rope_ready"), b + 1)
                pe.wait_ge(S("lz_ready"), b + 1)
                for blk in range(2):
                    nc.tensor.transpose(F0[:, P * blk:P * blk + P], QKR[j][:, 1, P * blk:P * blk + P], wt("ident"))
                    last = nc.tensor.transpose(F0[:, 2 * P + P * blk:3 * P + P * blk], vS[:, P * blk:P * blk + P],
                                               wt("ident"))
                last.then_inc(S("kvT_done"), 1)
                yield 14
                pe.wait_ge(S("kvT_ready"), b + 1)
                for blk in range(2):
                    last = mm(F0[:, 0:P], KVT[:, blk, :], KVT[:, 2 + blk, :], start=(blk == 0), stop=(blk == 1))
                last.then_inc(S("kv_done"), 1)

            def mid(b, j):
                for n in range(ROUNDS):
                    if n % 3 == 0:
                        yield (3, 5, 5)[n // 3]
                    if n == 0:
                        pe.wait_ge(S("v_shifted"), 16 * len(SHIFTS) * (b + 1))
                        wait(pe, "xl_ready", b)
                    at = 2 * (n // 3) * WP + 2 * (n % 3)
                    for q in range(Q):
                        img = V4[:, q, :].rearrange("p (h w) -> p h w", h=WP)
                        last = mm(F1[CM * q:CM * q + CM, 0:T], wpatch[:, ROUNDS * q + n, :],
                                  img[:, at // WP:at // WP + H, at % WP:at % WP + W],
                                  start=(n == 0), stop=(n == ROUNDS - 1))
                last.then_inc(S("lepe_done"), 1)
                yield 5
                pe.wait_ge(S("kvm_ready"), b + 1)
                pe.wait_ge(S("rope_ready"), b + 1)
                mm(F1[:, T:2 * T], KVM[j][:], QKR[j][:, 0, :], start=True, stop=True).then_inc(S("res_done"), 1)
                yield 6
                pe.wait_ge(S("u3_ready"), b + 1)
                mm(F1[:, 0:T], wt("wproj"), u3[:], start=True, stop=True).then_inc(S("proj_done"), 1)
                yield 8
                pe.wait_ge(S("gi_ready"), b + 1)
                mm(F1[:, T:T + 2], wt("groupsum"), gi[:], start=True, stop=True).then_inc(S("g2_done"), 1)
                yield 10
                pe.wait_ge(S("xg_ready"), b + 1)
                mm(F1[:, 0:T], wt("center"), xg[:], start=True, stop=True).then_inc(S("xc_done"), 1)
                yield 12
                pe.wait_ge(S("sq_ready"), b + 1)
                mm(F1[:, T:2 * T], wt("mean"), sq[:], start=True, stop=True).then_inc(S("var_done"), 1)

            def quarters(half):
                return XN4[:].rearrange("p (a h) t -> p a h t", h=2)[:, :, half, :]

            def tail(b, j):
                yield 2
                pe.wait_ge(S("xn_shifted"), 16 * DCONV * (b + 1))
                wait(pe, "bc_ready", b)
                for half in range(2):
                    last = mm(F2[DI * half:DI * half + DI, :], wtap[:], quarters(half), start=True, stop=True)
                last.then_inc(S("xp_done"), 1)
                yield 3
                pe.wait_ge(S("xs_ready"), b + 1)
                for half in range(2):
                    last = mm(F2[DI * half:DI * half + DI, :], wt("wz"), quarters(half), start=True, stop=True)
                last.then_inc(S("z_done"), 1)
                yield 4
                pe.wait_ge(S("zs_ready"), b + 1)
                mm(F2[:], wdt[:], flat(xs[j][:]), start=True, stop=True).then_inc(S("dt_done"), 1)
                yield 5
                pe.wait_ge(S("abs_ready"), b + 1)
                mm(F2[0:2 * 2 * DS, :], wt("wBC"), flat(xs[j][:]), start=True, stop=True).then_inc(S("bc_done"), 1)

            def back(b, j):
                yield 6
                pe.wait_ge(S("y2_ready"), b + 1)
                pe.wait_ge(S("f3_read"), b + 1)
                for qq in range(2):
                    last = mm(F3[:, 0:T], wt("wout", P * qq, P), y2[:, qq, :], start=(qq == 0), stop=(qq == 1))
                last.then_inc(S("wout_done"), 1)
                yield 8
                pe.wait_ge(S("y3_ready"), b + 1)
                mm(F3[:, 0:T], wt("center"), y3[:], start=True, stop=True).then_inc(S("xc2_done"), 1)
                yield 10
                pe.wait_ge(S("sq2_ready"), b + 1)
                mm(F3[:, T:2 * T], wt("mean"), sq2[:], start=True, stop=True).then_inc(S("var2_done"), 1)
                yield 14
                pe.wait_ge(S("xl2_ready"), b + 1)
                mm(F3[:, 0:T], wt("pw"), xl2[:], start=True, stop=True).then_inc(S("proj2_done"), 1)

            def broadcast_delta(u, j, g, half):
                wait(pe, "decay_ready", 2 * u + half)
                mm(D[:], pick[0:NPARTS * 32, g % 4, :], R[j][:, g // 4, 0, half, :],
                   start=True, stop=True).then_inc(S("delta_bc"), 1)

            def broadcast_du(u, j, g):
                wait(pe, "b_ready", u)
                for half in range(2):
                    last = mm(DU[:, half, :], pick[0:NPARTS * 32, g % 4, :], R[j][:, g // 4, 1, half, :],
                              start=True, stop=True)
                last.then_inc(S("du_bc"), 1)

            def collect(b, g):
                pe.wait_ge(S("hc_ready"), GROUPS * b + g + 1)
                if g == 0:
                    wait(pe, "y1_ready", b)
                for half in range(2):
                    last = mm(Y[64 * half:64 * half + 64, :], wt("place", DI * g, DI),
                              hst[g % 4][:, 512 * half:512 * half + 512], start=(g == 0), stop=(g == GROUPS - 1))
                last.then_inc(S("y_summed"), 1)

            def start():
                pe.wait_ge(S("regrouped"), 16 * 4 * NPARTS)
                for g in range(LEAD):
                    for half in range(2):
                        broadcast_delta(g, 0, g, half)
                    broadcast_du(g, 0, g)

            def unit(b, j, g, side, more):
                u, g2 = GROUPS * b + g + LEAD, (g + LEAD) % GROUPS
                j2 = j if g + LEAD < GROUPS else 1 - j
                for half in range(2):
                    side()
                    if g + LEAD < GROUPS or more:
                        if g + LEAD == GROUPS and half == 0:
                            pe.wait_ge(S("regrouped"), 16 * 4 * NPARTS * (b + 2))
                        broadcast_delta(u, j2, g2, half)
                        if half == 0:
                            broadcast_du(u, j2, g2)
                    if half == 0 and g >= LAG:
                        collect(b, g - LAG)
                    elif half == 0 and (not isinstance(b, int) or b > 0):
                        collect(b - 1, GROUPS + g - LAG)

            def finish():
                for g in range(GROUPS - LAG, GROUPS):
                    collect(B - 1, g)

            setup()
            periods(pe, (front, mid, tail, back), start, unit, finish, weights)

        @block.scalar
        def _(act):
            af = nc.scalar.activation
            act.dma_start(X[:, B // 2:, :], x_dram[:, B // 2:, :]).then_inc(S("x2_loaded"), 16)
            act.dma_start(W0s[:], w0).then_inc(S("w0_loaded"), 16)

            def setup():
                nc.scalar.preload_act_table_set("natural_log_exp_and_others")
                act.wait_ge(S("cc_loaded"), 16)
                act.wait_ge(S("gnv_ready"), 1)
                af(gln[:], gnv[:], ACT.Ln, bias=wt("eps"), scale=-1.0).then_inc(S("gln_ready"), 1)
                act.wait_ge(S("gln_ready"), 1)
                af(grs[:], gln[:], ACT.Exp, scale=-0.5).then_inc(S("grs_ready"), 1)
                act.wait_ge(S("w0_loaded"), 16)
                act.wait_ge(S("vpad_zero"), 1)
                act.wait_ge(S("borders_zero"), 6)

            def front(b, j):
                yield 2
                act.wait_ge(S("qk_done"), b + 1)
                for i in range(2):
                    bias, src = wt("bqkvo", i, 1), F0[:, T * i:T * i + T]
                    af(e_qk[:, i, :], src, ACT.Exp, bias=bias)
                    af(r_qk[:, i, :], src, ACT.Relu, bias=bias).then_inc(S("qk_act"), 1)
                yield 6
                act.wait_ge(S("vo_done"), b + 1)
                wait(act, "lepe_done", b)
                af(vpad[:, 0:WP * WP].rearrange("p (h w) -> p h w", h=WP)[:, PAD:PAD + H, PAD:PAD + W],
                   F0[:, 0:T].rearrange("p (h w) -> p h w", h=H),
                   ACT.Identity, bias=wt("bqkvo", 2, 1)).then_inc(S("vpad_ready"), 1)
                af(vS[:], F0[:, 0:T], ACT.Identity, bias=wt("bqkvo", 2, 1))
                wait(act, "u3_ready", b - 1)
                af(oS[j][:], F0[:, T:2 * T], ACT.Identity, bias=wt("bqkvo", 3, 1)).then_inc(S("o_ready"), 1)
                yield 9
                act.wait_ge(S("nmx_ready"), b + 1)
                af(Ex[:], F0[:, 0:T], ACT.Exp, bias=nmx[:], accum_out=sumE[:]).then_inc(S("exp_eff"), 1)
                yield 12
                act.wait_ge(S("den_done"), b + 1)
                wait(act, "u1_ready", b - 1)
                af(lz[:], F0[:, 0:T], ACT.Ln, bias=wt("zeps")).then_inc(S("lz_ready"), 1)
                act.wait_ge(S("lz_ready"), b + 1)
                af(zS[j][:], lz[:], ACT.Exp, scale=-1.0).then_inc(S("zS_ready"), 1)
                yield 13
                act.wait_ge(S("kvT_done"), b + 1)
                nc.scalar.copy(flat(KVT[:]), F0[:]).then_inc(S("kvT_ready"), 1)

            def mid(b, j):
                yield 7
                act.wait_ge(S("x1_ready"), b + 1)
                af(x1sq[:].unsqueeze(1), X[:, bass.ds(b, 1), :], ACT.Square, accum_out=gi[:, 1:2]).then_inc(
                    S("gi_ready"), 1)
                yield 9
                act.wait_ge(S("nv_ready"), b + 1)
                af(lnv[:], nv[:], ACT.Ln, bias=wt("eps"), scale=-1.0).then_inc(S("lnv_ready"), 1)
                act.wait_ge(S("lnv_ready"), b + 1)
                af(rs[:], lnv[:], ACT.Exp, scale=-0.5).then_inc(S("rs_ready"), 1)
                yield 11
                act.wait_ge(S("xc_done"), b + 1)
                af(sq[:], F1[:, 0:T], ACT.Square).then_inc(S("sq_ready"), 1)
                yield 12
                act.wait_ge(S("var_done"), b + 1)
                af(lr[:], F1[:, T:2 * T], ACT.Ln, bias=wt("eps")).then_inc(S("lr_ready"), 1)
                act.wait_ge(S("lr_ready"), b + 1)
                af(rr[:], lr[:], ACT.Exp, scale=-0.5).then_inc(S("rr_ready"), 1)

            def tail(b, j):
                yield 3
                act.wait_ge(S("xp_done"), b + 1)
                wait(act, "y1_ready", b - 1)
                af(flat(xs[j][:]), F2[:], ACT.Silu, bias=wt("convb")).then_inc(S("xs_ready"), 1)
                act.wait_ge(S("z_done"), b + 1)
                wait(act, "y2_ready", b - 1)
                af(flat(zs[j][:]), F2[:], ACT.Silu).then_inc(S("zs_ready"), 1)
                nc.scalar.preload_act_table_set("natural_log_exp_and_others")
                yield 4
                act.wait_ge(S("dt_done"), b + 1)
                wait(act, "delta_ready", b)
                af(rl[:], F2[:], ACT.Relu, bias=wt("bdt"))
                af(ab[:], F2[:], ACT.Abs, bias=wt("bdt")).then_inc(S("abs_ready"), 1)
                act.wait_ge(S("abs_ready"), b + 1)
                af(em[:], ab[:], ACT.Exp, scale=-1.0).then_inc(S("em_ready"), 1)
                act.wait_ge(S("em_ready"), b + 1)
                af(lnu[:], em[:], ACT.Ln, bias=1.0).then_inc(S("lnu_ready"), 1)
                yield 5
                act.wait_ge(S("bc_done"), b + 1)
                wait(act, "bc_copied", 16 * 2 * b)
                wait(act, "hc_ready", GROUPS * (b - 1))
                nc.scalar.copy(bc[:], F2[0:2 * 2 * DS, :]).then_inc(S("bc_ready"), 1)
                yield 5
                act.wait_ge(S("z_delta"), b + 1)
                wait(act, "regrouped", 16 * 4 * NPARTS * b)
                nc.scalar.copy(parts[0][:], Z[:]).then_inc(S("part0_ready"), 1)
                yield 7
                act.wait_ge(S("rem_ready"), b + 1)
                nc.scalar.copy(parts[1][:], Z[:]).then_inc(S("part1_ready"), 1)
                yield 10
                wait(act, "y3_ready", b - 1)
                af(xk[j][:], XN[j][:, DCONV - 1:], ACT.Copy, scale=wt("skip")).then_inc(S("xk_ready"), 1)

            def back(b, j):
                yield 8
                act.wait_ge(S("xc2_done"), b + 1)
                af(sq2[:], F3[:, 0:T], ACT.Square).then_inc(S("sq2_ready"), 1)
                yield 10
                act.wait_ge(S("var2_done"), b + 1)
                af(lr2[:], F3[:, T:2 * T], ACT.Ln, bias=wt("eps")).then_inc(S("lr2_ready"), 1)
                act.wait_ge(S("lr2_ready"), b + 1)
                af(rr2[:], lr2[:], ACT.Exp, scale=-0.5).then_inc(S("rr2_ready"), 1)

            def decay(u, g, half):
                if half == 0:
                    wait(act, "h_ready", u - 3)
                act.wait_ge(S("delta_bc"), 2 * u + half + 1)
                af(dec[g % 4][:, 2 * half:2 * half + 2, 1:T], D[:].rearrange("p (q t) -> p q t", q=2)[:, :, 1:T],
                   ACT.Exp, scale=negA[:, g:g + 1]).then_inc(S("decay_ready"), 1)

            def start():
                act.wait_ge(S("negA_ready"), 1)
                for g in range(LEAD):
                    for half in range(2):
                        decay(g, g, half)

            def unit(b, j, g, side, more):
                u, g2 = GROUPS * b + g + LEAD, (g + LEAD) % GROUPS
                for half in range(2):
                    side()
                    if g + LEAD < GROUPS or more:
                        decay(u, g2, half)

            def weights():
                act.wait_ge(S("w1_loaded"), 16)
                af(negA0[:], wt("alog"), ACT.Exp).then_inc(S("expA"), 1)

            setup()
            periods(act, (front, mid, tail, back), start, unit, lambda: None, weights)

        @block.gpsimd
        def _(pool):
            tt = nc.gpsimd.tensor_tensor
            nc.gpsimd.memset(vpad[:], 0.0).then_inc(S("vpad_zero"), 1)
            for j in range(2):
                nc.gpsimd.memset(XN[j][:, 0:DCONV - 1], 0.0).then_inc(S("borders_zero"), 1)
            for tile in dec:
                nc.gpsimd.memset(tile[:, :, 0:1], 0.0).then_inc(S("borders_zero"), 1)
            pool.wait_ge(S("w0_loaded"), 16)

            def front(b, j):
                yield 9
                pool.wait_ge(S("kk_ready"), b + 1)
                tt(t1[:], QK[:], wt("cos").unsqueeze(1).broadcast_to([P, 2, T]), ALU.mult).then_inc(S("t1_ready"), 1)
                yield 12
                pool.wait_ge(S("t1_ready"), b + 1)
                pool.wait_ge(S("t2_ready"), b + 1)
                wait(pool, "res_done", b - 1)
                tt(QKR[j][:], t1[:], t2[:], ALU.add).then_inc(S("rope_ready"), 1)

            def mid(b, j):
                yield 6
                pool.wait_ge(S("u2_ready"), b + 1)
                pool.wait_ge(S("o_ready"), b + 1)
                tt(u3[:], u2[:], oS[j][:], ALU.mult).then_inc(S("u3_ready"), 1)

            def tail(b, j):
                yield 8
                pool.wait_ge(S("rem_ready"), b + 1)
                pool.wait_ge(S("part1_ready"), b + 1)
                tt(parts[2][:], Z[:], parts[1][:], ALU.subtract).then_inc(S("part2_ready"), 1)

            def back(b, j):
                yield 2
                pool.wait_ge(S("y1_ready"), b + 1)
                tt(y2[:], y1[:], zs[j][:], ALU.mult).then_inc(S("y2_ready"), 1)

            def unit(b, j, g, side, more):
                side()
                u = GROUPS * b + g
                pool.wait_ge(S("h_ready"), u + 1)
                if g == 0:
                    pool.wait_ge(S("bc_copied"), 16 * 2 * (b + 1))
                tt(hst[g % 4][:], hst[g % 4][:], flat(Cs[j][:]), ALU.mult).then_inc(S("hc_ready"), 1)
                side()

            periods(pool, (front, mid, tail, back), lambda: None, unit, lambda: None)

        @block.vector
        def _(dve):
            v = nc.vector

            def setup():
                for b in range(B):
                    if b % (B // 2) == 0:
                        dve.wait_ge(S(("x_loaded", "x2_loaded")[b // (B // 2)]), 16)
                    v.bn_stats(gst[:, b, :], X[:, b, :]).then_inc(S("gst_ready"), 1)
                for b in range(B):
                    dve.wait_ge(S("gst_ready"), b + 1)
                    v.bn_aggr(gmv[:, b, :], gst[:, b, :]).then_inc(S("gmv_ready"), 1)
                dve.wait_ge(S("gmv_ready"), B)
                v.tensor_tensor(gnm[:], gmv[:, :, 0:1], gmv[:, :, 0:1], ALU.mult).then_inc(S("gsq_ready"), 1)
                v.tensor_copy(gin[:, :, 0:1], gmv[:, :, 0:1])
                dve.wait_ge(S("gsq_ready"), 1)
                v.tensor_tensor(gin[:, :, 1:2], gnm[:], gmv[:, :, 1:2], ALU.add).then_inc(S("gin_ready"), 1)
                dve.wait_ge(S("gavg_done"), 1)
                v.tensor_copy(gavg[:].rearrange("p b s -> p (b s)"), F0[:, 0:2 * B]).then_inc(S("gavg_ready"), 1)
                dve.wait_ge(S("gavg_ready"), 1)
                v.tensor_tensor(gnm[:], gavg[:, :, 0:1], gavg[:, :, 0:1], ALU.mult).then_inc(S("gsq_ready"), 1)
                dve.wait_ge(S("gsq_ready"), 2)
                v.tensor_tensor(gnv[:], gnm[:], gavg[:, :, 1:2], ALU.subtract).then_inc(S("gnv_ready"), 1)
                dve.wait_ge(S("grs_ready"), 1)
                v.scalar_tensor_tensor(out=gnm[:], in0=gavg[:, :, 0:1], scalar=-1.0, in1=grs[:], op0=ALU.mult,
                                       op1=ALU.mult).then_inc(S("gnm_ready"), 1)
                dve.wait_ge(S("gnm_ready"), 1)

            def weights():
                dve.wait_ge(S("w0_loaded"), 16)
                dve.wait_ge(S("w1_loaded"), 16)
                v.tensor_tensor(wpatch[:], wt("ident32").unsqueeze(1).broadcast_to([P, Q * ROUNDS, CM]),
                                wt("wlepe").unsqueeze(2).broadcast_to([P, Q * ROUNDS, CM]), ALU.mult)
                v.tensor_tensor(wtap[:], wt("wxp"), wt("convw"), ALU.mult)
                v.tensor_copy(pick[:].rearrange("p a m -> p (a m)"), wt("pick")).then_inc(S("weights_ready"), 1)
                dve.wait_ge(S("wprod_done"), 1)
                v.tensor_tensor(wdt[:], F3[:, 0:P], wt("half"), ALU.mult)
                v.tensor_tensor(bout[:], F3[:, P:P + 1], wt("pb"), ALU.add).then_inc(S("f3_read"), 1)
                dve.wait_ge(S("expA"), 1)
                v.tensor_scalar(negA[:], negA0[:], -1.0, None, ALU.mult).then_inc(S("negA_ready"), 1)
                dve.wait_ge(S("borders_zero"), 6)

            def front(b, j):
                yield 0
                wait(dve, "vo_done", b)
                v.tensor_scalar(xg0[:].unsqueeze(1), X[:, bass.ds(b, 1), :], grs[:, bass.ds(b, 1), :],
                                gnm[:, bass.ds(b, 1), :], ALU.mult, ALU.add).then_inc(S("xg0_ready"), 1)
                yield 4
                dve.wait_ge(S("qk_act"), 2 * b + 2)
                v.scalar_tensor_tensor(out=QK[:, 0, :], in0=e_qk[:, 0, :], scalar=1.0, in1=r_qk[:, 0, :],
                                       op0=ALU.min, op1=ALU.add, accum_out=qsum[:]).then_inc(S("q_ready"), 1)
                v.scalar_tensor_tensor(out=kraw[:], in0=e_qk[:, 1, :], scalar=1.0, in1=r_qk[:, 1, :],
                                       op0=ALU.min, op1=ALU.add).then_inc(S("k_ready"), 1)
                dve.wait_ge(S("q_ready"), b + 1)
                v.tensor_scalar(Mq[:], wt("headq"), qsum[:], None, ALU.mult).then_inc(S("mq_ready"), 1)
                yield 9
                dve.wait_ge(S("eff_done"), b + 1)
                v.tensor_reduce(nmx[:], F0[:, 0:T], AX_X, ALU.max, negate=True).then_inc(S("nmx_ready"), 1)
                yield 10
                dve.wait_ge(S("exp_eff"), b + 1)
                v.reciprocal(rE[:], sumE[:]).then_inc(S("rE_ready"), 1)
                dve.wait_ge(S("rE_ready"), b + 1)
                dve.wait_ge(S("k_ready"), b + 1)
                v.scalar_tensor_tensor(out=QK[:, 1, :], in0=Ex[:], scalar=rE[:], in1=kraw[:],
                                       op0=ALU.mult, op1=ALU.mult, accum_out=ksum[:]).then_inc(S("kk_ready"), 1)
                dve.wait_ge(S("kk_ready"), b + 1)
                v.tensor_scalar(Mk[:], wt("head"), ksum[:], None, ALU.mult).then_inc(S("mk_ready"), 1)
                yield 11
                dve.wait_ge(S("rot_done"), b + 1)
                v.tensor_tensor(t2[:], F0[:].rearrange("p (a t) -> p a t", a=2),
                                wt("sin").unsqueeze(1).broadcast_to([P, 2, T]), ALU.mult).then_inc(S("t2_ready"), 1)
                yield 15
                dve.wait_ge(S("kv_done"), b + 1)
                wait(dve, "res_done", b - 1)
                v.tensor_tensor(KVM[j][:], F0[:, 0:P], wt("head"), ALU.mult).then_inc(S("kvm_ready"), 1)

            def mid(b, j):
                yield 6
                dve.wait_ge(S("res_done"), b + 1)
                dve.wait_ge(S("zS_ready"), b + 1)
                v.tensor_tensor(u1[:], F1[:, T:2 * T], zS[j][:], ALU.mult).then_inc(S("u1_ready"), 1)
                dve.wait_ge(S("lepe_done"), b + 1)
                dve.wait_ge(S("u1_ready"), b + 1)
                v.scalar_tensor_tensor(out=u2[:], in0=F1[:, 0:T], scalar=wt("blepe"), in1=u1[:],
                                       op0=ALU.add, op1=ALU.add).then_inc(S("u2_ready"), 1)
                yield 7
                dve.wait_ge(S("proj_done"), b + 1)
                xb = X[:, bass.ds(b, 1), :]
                v.scalar_tensor_tensor(out=xb, in0=F1[:, 0:T].unsqueeze(1), scalar=wt("bproj"), in1=xb,
                                       op0=ALU.add, op1=ALU.add, accum_out=gi[:, 0:1]).then_inc(S("x1_ready"), 1)
                yield 9
                dve.wait_ge(S("g2_done"), b + 1)
                v.tensor_copy(ga[:], F1[:, T:T + 2]).then_inc(S("ga_ready"), 1)
                dve.wait_ge(S("ga_ready"), b + 1)
                v.scalar_tensor_tensor(out=nv[:], in0=ga[:, 0:1], scalar=ga[:, 0:1], in1=ga[:, 1:2],
                                       op0=ALU.mult, op1=ALU.subtract).then_inc(S("nv_ready"), 1)
                yield 10
                dve.wait_ge(S("rs_ready"), b + 1)
                v.tensor_scalar(nm[:], ga[:, 0:1], rs[:], -1.0, ALU.mult, ALU.mult).then_inc(S("nm_ready"), 1)
                dve.wait_ge(S("nm_ready"), b + 1)
                wait(dve, "xc_done", b)
                v.tensor_scalar(xg[:].unsqueeze(1), X[:, bass.ds(b, 1), :], rs[:], nm[:], ALU.mult,
                                ALU.add).then_inc(S("xg_ready"), 1)
                yield 13
                dve.wait_ge(S("rr_ready"), b + 1)
                v.scalar_tensor_tensor(out=xl[:], in0=F1[:, 0:T], scalar=wt("lnw"), in1=rr[:],
                                       op0=ALU.mult, op1=ALU.mult).then_inc(S("xl_ready"), 1)
                dve.wait_ge(S("xl_ready"), b + 1)
                wait(dve, "xk_ready", b - 1)
                wait(dve, "z_done", b)
                v.tensor_scalar(XN[j][:, DCONV - 1:], xl[:], wt("lnb"), None, ALU.add).then_inc(S("xn_ready"), 1)

            def tail(b, j):
                yield 6
                dve.wait_ge(S("em_ready"), b + 1)
                v.tensor_scalar(um1[:], em[:], 1.0, None, ALU.add).then_inc(S("um1_ready"), 1)
                dve.wait_ge(S("um1_ready"), b + 1)
                v.scalar_tensor_tensor(out=cor[:], in0=um1[:], scalar=1.0, in1=em[:],
                                       op0=ALU.subtract, op1=ALU.subtract).then_inc(S("cor_ready"), 1)
                dve.wait_ge(S("cor_ready"), b + 1)
                dve.wait_ge(S("lnu_ready"), b + 1)
                v.tensor_tensor(dl1[:], lnu[:], cor[:], ALU.subtract).then_inc(S("dl1_ready"), 1)
                yield 6
                dve.wait_ge(S("dl1_ready"), b + 1)
                wait(dve, "part2_ready", b)
                v.tensor_tensor(Z[:, 0, :], dl1[:], rl[:], ALU.add).then_inc(S("delta_ready"), 1)
                dve.wait_ge(S("delta_ready"), b + 1)
                v.tensor_tensor(Z[:, 1, :], Z[:, 0, :], flat(xs[j][:]), ALU.mult).then_inc(S("z_delta"), 1)
                yield 7
                dve.wait_ge(S("z_delta"), b + 1)
                dve.wait_ge(S("part0_ready"), b + 1)
                v.tensor_tensor(Z[:], Z[:], parts[0][:], ALU.subtract).then_inc(S("rem_ready"), 1)

            def back(b, j):
                yield 2
                dve.wait_ge(S("y_summed"), GROUPS * (b + 1))
                v.scalar_tensor_tensor(out=flat(y1[:]), in0=flat(xs[j][:]), scalar=wt("D"), in1=Y[:],
                                       op0=ALU.mult, op1=ALU.add).then_inc(S("y1_ready"), 1)
                yield 8
                dve.wait_ge(S("wout_done"), b + 1)
                dve.wait_ge(S("xk_ready"), b + 1)
                v.tensor_tensor(y3[:], xk[j][:], F3[:, 0:T], ALU.add).then_inc(S("y3_ready"), 1)
                yield 13
                dve.wait_ge(S("rr2_ready"), b + 1)
                v.scalar_tensor_tensor(out=xl2[:], in0=F3[:, 0:T], scalar=wt("lnw"), in1=rr2[:],
                                       op0=ALU.mult, op1=ALU.mult).then_inc(S("xl2_ready"), 1)
                yield 15
                dve.wait_ge(S("proj2_done"), b + 1)
                xb = X[:, bass.ds(b, 1), :]
                v.scalar_tensor_tensor(out=xb, in0=F3[:, 0:T].unsqueeze(1), scalar=bout[:], in1=xb,
                                       op0=ALU.add, op1=ALU.add).then_inc(S("f3_read"), 1)

            def times_b(b, u, j, g):
                dve.wait_ge(S("du_bc"), u + 1)
                if g == 0:
                    dve.wait_ge(S("bc_copied"), 16 * 2 * (b + 1))
                wait(dve, "h_ready", u - 1)
                v.tensor_tensor(bin_[g % 2][:], flat(DU[:]), flat(Bs[j][:]), ALU.mult).then_inc(S("b_ready"), 1)

            def unit(b, j, g, side, more):
                u = GROUPS * b + g
                if g + 1 < GROUPS:
                    times_b(b, u + 1, j, g + 1)
                elif more:
                    times_b(b + 1, u + 1, 1 - j, 0)
                side()
                dve.wait_ge(S("b_ready"), u + 1)
                dve.wait_ge(S("decay_ready"), 2 * u + 2)
                wait(dve, "y_summed", u - 3)
                v.tensor_tensor_scan(hst[g % 4][:], flat(dec[g % 4][:]), bin_[g % 2][:], 0.0,
                                     ALU.mult, ALU.add).then_inc(S("h_ready"), 1)
                side()

            setup()
            periods(dve, (front, mid, tail, back), lambda: times_b(0, 0, 0, 0), unit, lambda: None, weights)


def kernel(**inputs):
    import numpy as np
    import concourse.bacc as bacc
    from concourse.bass_utils import run_bass_kernel_spmd as run

    a = {k: np.asarray(v) for k, v in inputs.items()}
    f = np.float32

    def pack(table, cols, named):
        out = np.zeros((P, cols), f)
        for name, block in named.items():
            start, width = table[name]
            out[:block.shape[0], start:start + width] = block.reshape(block.shape[0], width)
        return out

    def col(v):
        return v.reshape(-1, 1)

    wlepe = np.zeros((2, 2, CM, Q, 3, 3), f)
    w5 = np.zeros((C, 6, 6), f)
    w5[:, :KS, :KS] = a["L0_conv_w_lepe"][:, 0]
    wlepe[:] = w5.reshape(Q, CM, 3, 2, 3, 2).transpose(3, 5, 1, 0, 2, 4)
    wlepe = wlepe.reshape(P, Q * ROUNDS)

    w0 = pack(W0, W0_COLS, {
        "wqkvo": a["L0_conv_w_qkvo"].T, "bqkvo": a["L0_conv_b_qkvo"].reshape(4, C).T,
        "wlepe": wlepe, "blepe": col(a["L0_conv_b_lepe"]),
        "wproj": a["L0_conv_w_proj"].T, "bproj": col(a["L0_conv_b_proj"]),
        "cos": np.tile(a["L0_conv_cos"].T, (HEADS, 1)), "sin": np.tile(a["L0_conv_sin"].T, (HEADS, 1))})

    W_in, W_x, W_out = a["L1_conv_W_in"], a["L1_conv_W_x"], a["L1_conv_W_out"]
    wout = np.zeros((P, 2, P), f)
    wz = np.zeros((DCONV, CM, DI), f)
    wz[DCONV - 1] = W_in[DI:].T
    for qq in range(2):
        for half in range(2):
            c, m = slice(CM * (2 * qq + half), CM * (2 * qq + half) + CM), slice(DI * half, DI * half + DI)
            wout[m, qq, c] = W_out.T
    wbc = np.zeros((2, DI, 2, 2 * DS), f)
    for half in range(2):
        wbc[half, :, half] = W_x[DTR:].T
    wbc = wbc.reshape(P, 2 * 2 * DS)
    both = lambda v: np.concatenate([v, v], 0)
    w1 = pack(W1, W1_COLS, {
        "lnw": col(a["L1_conv_norm_w"]), "lnb": col(a["L1_conv_norm_b"]), "wxp": np.tile(W_in[:DI].T, (DCONV, 1)), "wz": wz.reshape(P, DI),
        "convw": np.repeat(a["L1_conv_conv_w"][:, 0, :].T, CM, 0),
        "convb": col(both(a["L1_conv_conv_b"])),
        "wBC": wbc,
        "wdt_in": both(W_x[:DTR].T).T, "wdt_out": both(a["L1_conv_W_dt"]).T, "bdt": col(both(a["L1_conv_b_dt"])),
        "alog": a["L1_conv_A_log"].reshape(GROUPS, DD * DS).T, "D": col(both(a["L1_conv_D"])), "wout": wout,
        "pw": a["L1_conv_proj_w"].T, "pb": col(a["L1_conv_proj_b"]),
        "skip": np.broadcast_to(a["L1_conv_skip_scale"].reshape(1, 1), (P, 1))})

    c = np.arange(P)
    ident = np.eye(P, dtype=f)
    head = (c[:, None] // HD == c[None] // HD).astype(f)
    rot = np.zeros((P, P), f)
    rot[c[1::2], c[0::2]] = -1
    rot[c[0::2], c[1::2]] = 1
    pick = np.zeros((NPARTS, 32, 4, P), f)
    place = np.zeros((P, GROUPS, DI), f)
    for g in range(GROUPS):
        place[c, g, DD * g + c // DS] = 1
    for s in range(4):
        pick[:, DD * s + c // DS, s, c] = 1
    cc = pack(CC, CC_COLS, {
        "ident": ident, "head": head, "headq": head * f(HD ** -0.5 / T), "rot": rot,
        "group": (c[:, None] // 4 == c[None] // 4).astype(f) / 4,
        "groupsum": (c[:, None] // 4 == c[None] // 4).astype(f) / (4 * T), "center": ident - f(1 / C),
        "mean": np.full((P, P), 1 / C, f), "zeps": np.full((P, 1), 1e-6, f),
        "half": (c[:, None] // DI == c[None] // DI).astype(f), "eps": np.full((P, 1), LN_EPS, f),
        "ident32": ident[:, :CM] + ident[:, CM:2 * CM] + ident[:, 2 * CM:3 * CM] + ident[:, 3 * CM:],
        "pick": pick.reshape(NPARTS * 32, 4 * P), "place": place})

    nc = bacc.Bacc("TRN2", target_bir_lowering=False, num_devices=1)
    arrays, args = {}, []
    for name, v in (("x", a["x"]), ("w0", w0), ("w1", w1), ("cc", cc)):
        arrays[name] = np.ascontiguousarray(v)
        args.append(nc.dram_tensor(name, v.shape, mybir.dt.from_np(v.dtype), kind="ExternalInput").ap())
    out = nc.dram_tensor("out", (B, C, H, W), F32, kind="ExternalOutput").ap()
    block_kernel(nc, *args, out)
    r = run(nc, [arrays], core_ids=[0])
    return r.results[0]["out"]
```

```python
from contextlib import ExitStack

import concourse.bass as bass
from concourse import mybir

F32 = mybir.dt.float32
BF16 = mybir.dt.bfloat16
ALU = mybir.AluOpType
ACT = mybir.ActivationFunctionType
AX_X = mybir.AxisListType.X

P = 128
B, C, H, W = 8, 128, 16, 16
T = H * W
HEADS, HD = 8, 16
Q, CM = 4, 32
DI, DS, DCONV, DTR = 64, 16, 4, 2
GROUPS, DD = 8, 8
KS, PAD = 5, 2
WP = W + 2 * PAD
PATCH = ((0, 0), (0, 1), (0, 3), (1, 3))
PLACES = ((0, 0), (0, 1), (1, -1), (1, 1), (2, 0), (3, -1), (3, 1), (4, 0))
ROUNDS = len(PLACES)
SHIFTS = [y * WP + x for y, x in PATCH]
GN_EPS = LN_EPS = 1e-5
NPARTS = 3


def columns(widths):
    at, out = 0, {}
    for name, width in widths:
        out[name] = (at, width)
        at += width
    return out, at


W0, W0_COLS = columns([("wqkvo", 4 * C), ("bqkvo", 4), ("wlepe", Q * ROUNDS), ("blepe", 1), ("wproj", C),
                       ("bproj", 1), ("cos", T), ("sin", T)])
W1, W1_COLS = columns([("lnw", 1), ("lnb", 1), ("wxp", DI), ("wz", DI), ("convw", DI), ("convb", 1),
                       ("wBC", 2 * 2 * DS), ("wdt_in", P), ("wdt_out", P), ("bdt", 1), ("alog", GROUPS), ("D", 1),
                       ("wout", 2 * P), ("pw", C), ("pb", 1), ("skip", 1)])
CC, CC_COLS = columns([("group", P), ("eps", 1), ("ident", P), ("head", P), ("headq", P), ("rot", P), ("groupsum", P),
                       ("center", P), ("mean", P), ("half", P), ("zeps", 1), ("pick", 4 * P), ("place", P),
                       ("ident32", CM)])


def block_kernel(nc, x, w0, w1, cc, out):
    with ExitStack() as ctx:
        def sb(name, shape, dt=F32):
            return ctx.enter_context(nc.sbuf_tensor(name, shape, dt))

        sems = {}

        def S(name):
            if name not in sems:
                sems[name] = ctx.enter_context(nc.semaphore(name))
            return sems[name]

        X = sb("X", [P, B, T])
        W0s, W1s, CCs = sb("W0s", [P, W0_COLS]), sb("W1s", [P, W1_COLS]), sb("CCs", [P, CC_COLS])
        gst, gmv, gin = sb("gst", [P, B, 6]), sb("gmv", [P, B, 2]), sb("gin", [P, B, 2])
        gavg, gnv, gln, grs, gsq = (sb(n, [P, B, w]) for n, w in
                                    (("gavg", 2), ("gnv", 1), ("gln", 1), ("grs", 1), ("gsq", 1)))
        wpatch = sb("wpatch", [P, Q * ROUNDS, CM])
        wtap = sb("wtap", [P, DI])
        wdt = sb("wdt", [P, P])
        negA0, negA = sb("negA0", [P, GROUPS]), sb("negA", [P, GROUPS])
        bout = sb("bout", [P, 1])
        cwout = sb("cwout", [P, 2, P])
        dsel = sb("dsel", [P, 4, CM])
        pick = sb("pick", [P, 4, P], BF16)

        xg0, e_qk, r_qk = sb("xg0", [P, T]), sb("e_qk", [P, 2, T]), sb("r_qk", [P, 2, T])
        QK, kraw = sb("QK", [P, 2, T]), sb("kraw", [P, T])
        qsum, Mq, nmx, Ex, sumE, rE, ksum, Mk = (sb(n, [P, w]) for n, w in (
            ("qsum", 1), ("Mq", P), ("nmx", 1), ("Ex", T), ("sumE", 1), ("rE", 1), ("ksum", 1), ("Mk", P)))
        vS, oS = sb("vS", [P, T]), [sb(f"oS_{j}", [P, T]) for j in range(2)]
        vpad = sb("vpad", [P, WP * WP + SHIFTS[-1]])
        V4 = sb("V4", [P, Q, WP * WP])
        t1, t2 = sb("t1", [P, 2, T]), sb("t2", [P, 2, T])
        QKR = [sb(f"QKR_{j}", [P, 2, T]) for j in range(2)]
        lz, zS = sb("lz", [P, T]), [sb(f"zS_{j}", [P, T]) for j in range(2)]
        KVT, KVM = sb("KVT", [P, 4, P]), [sb(f"KVM_{j}", [P, P]) for j in range(2)]
        u1, u2, u3 = sb("u1", [P, T]), sb("u2", [P, T]), sb("u3", [P, T])
        x1sq, gi, ga, nv, lnv, rs = (sb(n, [P, w]) for n, w in (
            ("x1sq", T), ("gi", 2), ("ga", 2), ("nv", 1), ("lnv", 1), ("rs", 1)))
        xg, sq, lr, rr, xl = (sb(n, [P, T]) for n in ("xg", "sq", "lr", "rr", "xl"))
        XN = [sb(f"XN_{j}", [P, DCONV - 1 + T]) for j in range(2)]
        XN4 = sb("XN4", [P, Q, T])
        xk = [sb(f"xk_{j}", [P, T]) for j in range(2)]
        xs = [sb(f"xs_{j}", [P, 2, T]) for j in range(2)]
        zs = [sb(f"zs_{j}", [P, 2, T]) for j in range(2)]
        ab, rl, em, lnu, um1, cor, dl1 = (sb(n, [P, 2 * T]) for n in ("ab", "rl", "em", "lnu", "um1", "cor", "dl1"))
        Z = sb("Z", [P, 2, 2 * T])
        parts = [sb(f"part{i}", [P, 2, 2 * T], BF16) for i in range(NPARTS)]
        R = [sb(f"R_{j}", [NPARTS * 32, 2, 2, 2, 2 * T], BF16) for j in range(2)]
        bc = sb("bc", [2 * 2 * DS, 2 * T])
        Bs = [sb(f"Bs_{j}", [P, 2, 2 * T]) for j in range(2)]
        Cs = [sb(f"Cs_{j}", [P, 2, 2 * T]) for j in range(2)]
        dec = [sb(f"dec_{j}", [P, 4, T]) for j in range(4)]
        bin_ = [sb(f"bin_{j}", [P, 4 * T]) for j in range(2)]
        hst = [sb(f"hst_{j}", [P, 4 * T]) for j in range(4)]
        y2 = sb("y2", [P, 2, T])
        sq2, lr2, rr2, xl2 = (sb(n, [P, T]) for n in ("sq2", "lr2", "rr2", "xl2"))

        F0, F1, F2, F3, Y, D = (ctx.enter_context(nc.psum_tensor(n, [P, 512], F32))
                                for n in ("F0", "F1", "F2", "F3", "Y", "D"))
        DU = ctx.enter_context(nc.psum_tensor("DU", [P, 2, 512], F32))

        def flat(ap):
            return ap.rearrange("p a t -> p (a t)")

        def wt(name, i=0, n=None, rows=P):
            for tile, table in ((W0s, W0), (W1s, W1), (CCs, CC)):
                if name in table:
                    a, w = table[name]
                    n = w if n is None else n
                    return tile[0:rows, a + i:a + i + n]

        def wait(eng, name, count):
            if not isinstance(count, int) or count > 0:
                eng.wait_ge(S(name), count)

        def begin(chain, b, j, at=0):
            steps = chain(b, j)
            return [steps, at + next(steps, IDLE), at]

        def segment(works, s):
            for work in works:
                while work[1] == s:
                    work[1] = work[2] + next(work[0], IDLE)

        def periods(eng, chains, start, unit, finish):
            weights, front, mid, tail, back = chains

            def run(works, last):
                for s in range(last):
                    segment(works, s)

            def period(b, j, ahead=3, behind=True):
                works = []
                if behind:
                    works.append(begin(back, b - 1, 1 - j))
                if ahead > 0:
                    works.append(begin(tail, b + 1, 1 - j))
                if ahead > 1:
                    works.append(begin(mid, b + 2, j))
                if ahead > 2:
                    works.append(begin(front, b + 3, 1 - j))
                for g in range(GROUPS):
                    seg = iter(range(SIDES * g, SIDES * (g + 1)))
                    unit(b, j, g, lambda: segment(works, next(seg)), ahead > 0)

            f, m, t, w = PROLOGUE
            run([begin(tail, 0, 0, t[0]), begin(mid, 0, 0, m[0]), begin(mid, 1, 1, m[1]), begin(front, 0, 0, f[0]),
                 begin(front, 1, 1, f[1]), begin(front, 2, 0, f[2]), begin(weights, 0, 0, w[0])], 5 * SEGMENTS)
            start()
            period(0, 0, behind=False)
            with eng.Fori(0, (B - 4) // 2) as pair:
                period(2 * pair + 1, 1)
                period(2 * pair + 2, 0)
            for left in (2, 1, 0):
                period(B - 1 - left, (B - 1 - left) % 2, ahead=left)
            finish()
            run([begin(back, B - 1, 1)], SEGMENTS)

        SIDES = 4
        SEGMENTS = SIDES * GROUPS
        IDLE = 100 * SEGMENTS
        PROLOGUE = ((18, 48, 88), (48, 88), (90,), (29,))
        LAG = 1
        LEAD = 2
        v_dram = nc.dram_tensor("v_scratch", [P, WP * WP + SHIFTS[-1]], F32).ap()
        xn_dram = nc.dram_tensor("xn_scratch", [P, DCONV - 1 + T], F32).ap()
        bc_dram = nc.dram_tensor("bc_scratch", [2, DS, 2 * 2 * T], F32).ap()
        x_dram = x.rearrange("b c h w -> c b (h w)")
        out_dram = out.rearrange("b c h w -> c b (h w)")
        block = ctx.enter_context(nc.Block())

        @block.sync
        def _(sp):
            sp.dma_start(X[:, 0:1, :], x_dram[:, 0:1, :]).then_inc(S("x0_loaded"), 16)
            cc_first = CC["ident"][0]
            sp.dma_start(CCs[:, 0:cc_first], cc[:, 0:cc_first]).then_inc(S("group_loaded"), 16)
            cc_split = CC["pick"][0]
            sp.dma_start(CCs[:, cc_first:cc_split], cc[:, cc_first:cc_split]).then_inc(S("cc_loaded"), 16)
            sp.dma_start(X[:, 1:, :], x_dram[:, 1:, :]).then_inc(S("x_loaded"), 16)
            sp.dma_start(CCs[:, cc_split:], cc[:, cc_split:]).then_inc(S("w1_loaded"), 16)
            sp.dma_start(W1s[:], w1).then_inc(S("w1_loaded"), 16)

            def front(b, j):
                yield 4
                sp.wait_ge(S("vpad_ready"), b + 1)
                sp.dma_start(v_dram, vpad[:]).then_inc(S("v_out"), 16)
                yield 18
                sp.wait_ge(S("v_out"), 16 * (b + 1))
                for n, off in enumerate(SHIFTS):
                    sp.dma_start(V4[CM * n:CM * n + CM, :, :],
                                 v_dram[:, off:off + WP * WP].rearrange("(q c) n -> c q n", q=Q)).then_inc(
                                     S("v_shifted"), 16)

            def mid(b, j):
                yield 24
                sp.wait_ge(S("xn_ready"), b + 1)
                sp.dma_start(xn_dram, XN[j][:]).then_inc(S("xn_out"), 16)
                yield 24
                sp.wait_ge(S("xn_out"), 16 * (b + 1))
                for k in range(DCONV):
                    sp.dma_start(XN4[CM * k:CM * k + CM, :, :],
                                 xn_dram[:, k:k + T].rearrange("(q c) t -> c q t", q=Q)).then_inc(S("xn_shifted"), 16)

            def tail(b, j):
                yield 0
                sp.wait_ge(S("bc_ready"), b + 1)
                sp.dma_start(bc_dram.rearrange("w s (h n) -> h (w s) n", h=2), bc[:]).then_inc(S("bc_out"), 16)
                yield 4
                sp.wait_ge(S("bc_out"), 16 * (b + 1))
                for which, copies in enumerate((Bs[j], Cs[j])):
                    sp.dma_start(flat(copies[:]), bc_dram[which].unsqueeze(0).broadcast_to(
                        [DD, DS, 2 * 2 * T])).then_inc(S("bc_copied"), 16)
                for i in range(NPARTS):
                    yield (16, 16, 16)[i]
                    sp.wait_ge(S(f"part{i}_ready"), b + 1)
                    for half in range(2):
                        for kg in range(2):
                            p0 = 64 * half + 32 * kg
                            sp.dma_start(R[j][32 * i:32 * i + 32, kg, :, half, :],
                                         parts[i][p0:p0 + 32, :, :]).then_inc(S("regrouped"), 16)

            def back(b, j):
                yield 31
                sp.wait_ge(S("f3_read"), b + 2)
                sp.dma_start(out_dram[:, bass.ds(b, 1), :], X[:, bass.ds(b, 1), :]).then_inc(S("stored"), 16)

            def unit(b, j, g, side, more):
                for _ in range(SIDES):
                    side()

            def weights(b, j):
                yield from ()

            periods(sp, (weights, front, mid, tail, back), lambda: None, unit, lambda: None)
            sp.wait_ge(S("stored"), 16 * B)

        @block.tensor
        def _(pe):
            mm = nc.tensor.matmul

            def setup():
                pe.wait_ge(S("group_loaded"), 16)
                averages(0, 0, 1, F0)
                pe.wait_ge(S("cc_loaded"), 16)
                pe.wait_ge(S("wqkvo_loaded"), 16)

            def averages(k, lo, hi, bank):
                pe.wait_ge(S("gin_ready"), k + 1)
                mm(bank[:, 0:2 * (hi - lo)], wt("group"), gin[:, lo:hi, :].rearrange("p b s -> p (b s)"),
                   start=True, stop=True).then_inc(S("gavg_done"), 1)

            def weights(b, j):
                yield 3
                averages(1, 1, B, F3)
                yield 9
                pe.wait_ge(S("gavg_ready"), 2)
                pe.wait_ge(S("w0_loaded"), 16)
                pe.wait_ge(S("w1_loaded"), 32)
                mm(F3[:, 0:P], wt("wdt_in", rows=DTR), wt("wdt_out", rows=DTR), start=True, stop=True)
                mm(F3[:, P:P + 1], wt("pw"), wt("lnb"), start=True, stop=True)
                for kg in range(2):
                    last = mm(F3[:, T + P * kg:T + P * kg + P], wt("wout", P * kg, P), wt("center"),
                              start=True, stop=True)
                last.then_inc(S("wprod_done"), 1)

            def front(b, j):
                yield 1
                pe.wait_ge(S("xg0_ready"), b + 1)
                wait(pe, "kvm_ready", b)
                for i in range(2):
                    last = mm(F0[:, T * i:T * i + T], wt("wqkvo", C * i, C), xg0[:], start=True, stop=True)
                last.then_inc(S("qk_done"), 1)
                yield 8
                pe.wait_ge(S("qk_act"), 2 * b + 2)
                for i in range(2):
                    last = mm(F0[:, T * i:T * i + T], wt("wqkvo", C * (2 + i), C), xg0[:], start=True, stop=True)
                last.then_inc(S("vo_done"), 1)
                yield 12
                pe.wait_ge(S("k_ready"), b + 1)
                pe.wait_ge(S("mq_ready"), b + 1)
                pe.wait_ge(S("o_ready"), b + 1)
                mm(F0[:, 0:T], Mq[:], kraw[:], start=True, stop=True).then_inc(S("eff_done"), 1)
                yield 19
                pe.wait_ge(S("kk_ready"), b + 1)
                mm(F0[:], wt("rot"), flat(QK[:]), start=True, stop=True).then_inc(S("rot_done"), 1)
                yield 20
                pe.wait_ge(S("mk_ready"), b + 1)
                pe.wait_ge(S("t2_ready"), b + 1)
                mm(F0[:, 0:T], Mk[:], QK[:, 0, :], start=True, stop=True).then_inc(S("den_done"), 1)
                yield 28
                pe.wait_ge(S("rope_ready"), b + 1)
                pe.wait_ge(S("lz_ready"), b + 1)
                for blk in range(2):
                    nc.tensor.transpose(F0[:, P * blk:P * blk + P], QKR[j][:, 1, P * blk:P * blk + P], wt("ident"))
                    last = nc.tensor.transpose(F0[:, 2 * P + P * blk:3 * P + P * blk], vS[:, P * blk:P * blk + P],
                                               wt("ident"))
                last.then_inc(S("kvT_done"), 1)
                yield 30
                pe.wait_ge(S("kvT_ready"), b + 1)
                for blk in range(2):
                    last = mm(F0[:, 0:P], KVT[:, blk, :], KVT[:, 2 + blk, :], start=(blk == 0), stop=(blk == 1))
                last.then_inc(S("kv_done"), 1)

            def mid(b, j):
                for n, (dy, dx) in enumerate(PLACES):
                    yield (0, 0, 4, 5, 6, 6, 7, 7)[n]
                    if n == 0:
                        pe.wait_ge(S("weights_ready"), 1)
                        pe.wait_ge(S("v_shifted"), 16 * len(SHIFTS) * (b + 1))
                        wait(pe, "xl_ready", b)
                    at = dy * WP + dx
                    for q in range(Q):
                        img = V4[:, q, at:at + H * WP].rearrange("p (h w) -> p h w", h=H)
                        last = mm(F1[CM * q:CM * q + CM, 0:T], wpatch[:, ROUNDS * q + n, :],
                                  img[:, :, 0:W],
                                  start=(n == 0), stop=(n == ROUNDS - 1))
                last.then_inc(S("lepe_done"), 1)
                yield 8
                pe.wait_ge(S("kvm_ready"), b + 1)
                pe.wait_ge(S("rope_ready"), b + 1)
                mm(F1[:, T:2 * T], KVM[j][:], QKR[j][:, 0, :], start=True, stop=True).then_inc(S("res_done"), 1)
                yield 12
                pe.wait_ge(S("u3_ready"), b + 1)
                mm(F1[:, 0:T], wt("wproj"), u3[:], start=True, stop=True).then_inc(S("proj_done"), 1)
                yield 15
                pe.wait_ge(S("gi_ready"), b + 1)
                mm(F1[:, T:T + 2], wt("groupsum"), gi[:], start=True, stop=True).then_inc(S("g2_done"), 1)
                yield 19
                pe.wait_ge(S("xg_ready"), b + 1)
                mm(F1[:, 0:T], wt("center"), xg[:], start=True, stop=True).then_inc(S("xc_done"), 1)
                yield 20
                pe.wait_ge(S("sq_ready"), b + 1)
                mm(F1[:, T:2 * T], wt("mean"), sq[:], start=True, stop=True).then_inc(S("var_done"), 1)

            def quarters(half):
                return XN4[:].rearrange("p (a h) t -> p a h t", h=2)[:, :, half, :]

            def tail(b, j):
                yield 4
                pe.wait_ge(S("xn_shifted"), 16 * DCONV * (b + 1))
                wait(pe, "bc_ready", b)
                for half in range(2):
                    last = mm(F2[DI * half:DI * half + DI, :], wtap[:], quarters(half), start=True, stop=True)
                last.then_inc(S("xp_done"), 1)
                yield 5
                pe.wait_ge(S("xs_ready"), b + 1)
                for kg in range(2):
                    for i in range(Q):
                        half, qq = divmod(i, 2)
                        last = mm(F2[CM * i:CM * i + CM, T * kg:T * kg + T], wt("wz", CM * kg, CM),
                                  XN4[:, 2 * qq + half, :], start=True, stop=True)
                last.then_inc(S("z_done"), 1)
                yield 6
                pe.wait_ge(S("f3_read"), 1)
                pe.wait_ge(S("zs_ready"), b + 1)
                mm(F2[:], wdt[:], flat(xs[j][:]), start=True, stop=True).then_inc(S("dt_done"), 1)
                yield 7
                pe.wait_ge(S("abs_ready"), b + 1)
                mm(F2[0:2 * 2 * DS, :], wt("wBC"), flat(xs[j][:]), start=True, stop=True).then_inc(S("bc_done"), 1)

            def back(b, j):
                yield 16
                pe.wait_ge(S("y2_ready"), b + 1)
                pe.wait_ge(S("xk_ready"), b + 1)
                pe.wait_ge(S("f3_read"), b + 1)
                for kg in range(2):
                    mm(F3[:, 0:T], cwout[:, kg, :], y2[:, kg, :], start=(kg == 0), stop=False)
                mm(F3[:, 0:T], wt("center"), xk[j][:], start=False, stop=True).then_inc(S("xc2_done"), 1)
                yield 24
                pe.wait_ge(S("sq2_ready"), b + 1)
                mm(F3[:, T:2 * T], wt("mean"), sq2[:], start=True, stop=True).then_inc(S("var2_done"), 1)
                yield 28
                pe.wait_ge(S("xl2_ready"), b + 1)
                mm(F3[:, 0:T], wt("pw"), xl2[:], start=True, stop=True).then_inc(S("proj2_done"), 1)

            def broadcast_delta(u, j, g, half):
                wait(pe, "decay_ready", 2 * u + half)
                mm(D[:], pick[0:NPARTS * 32, g % 4, :], R[j][:, g // 4, 0, half, :],
                   start=True, stop=True).then_inc(S("delta_bc"), 1)

            def broadcast_du(u, j, g):
                wait(pe, "b_ready", u)
                for half in range(2):
                    last = mm(DU[:, half, :], pick[0:NPARTS * 32, g % 4, :], R[j][:, g // 4, 1, half, :],
                              start=True, stop=True)
                last.then_inc(S("du_bc"), 1)

            def collect(b, j, g):
                pe.wait_ge(S("hc_ready"), GROUPS * b + g + 1)
                if g == 0:
                    wait(pe, "y2_ready", b)
                kg = g // 4
                if g % 4 == 0:
                    for i in range(Q):
                        half, qq = divmod(i, 2)
                        mm(Y[CM * i:CM * i + CM, T * kg:T * kg + T], dsel[:, 2 * half + kg, :], xs[j][:, qq, :],
                           start=True, stop=False)
                for i in range(Q):
                    last = mm(Y[CM * i:CM * i + CM, T * kg:T * kg + T], wt("place", CM * (g % 4), CM),
                              hst[g % 4][:, T * i:T * i + T], start=False, stop=(g % 4 == 3))
                last.then_inc(S("y_summed"), 1)

            def start():
                pe.wait_ge(S("regrouped"), 16 * 4 * NPARTS)
                for g in range(LEAD):
                    broadcast_delta(g, 0, g, 0)
                    broadcast_du(g, 0, g)
                    broadcast_delta(g, 0, g, 1)

            def unit(b, j, g, side, more):
                u, g2 = GROUPS * b + g + LEAD, (g + LEAD) % GROUPS
                j2 = j if g + LEAD < GROUPS else 1 - j
                ahead = g + LEAD < GROUPS or more
                side()
                if ahead:
                    if g + LEAD == GROUPS:
                        pe.wait_ge(S("regrouped"), 16 * 4 * NPARTS * (b + 2))
                    broadcast_delta(u, j2, g2, 0)
                side()
                if ahead:
                    broadcast_du(u, j2, g2)
                side()
                if g >= LAG:
                    collect(b, j, g - LAG)
                elif not isinstance(b, int) or b > 0:
                    collect(b - 1, 1 - j, GROUPS + g - LAG)
                side()
                if ahead:
                    broadcast_delta(u, j2, g2, 1)

            def finish():
                for g in range(GROUPS - LAG, GROUPS):
                    collect(B - 1, 1, g)

            setup()
            periods(pe, (weights, front, mid, tail, back), start, unit, finish)

        @block.scalar
        def _(act):
            af = nc.scalar.activation
            w0_split = W0["wlepe"][0]
            act.dma_start(W0s[:, 0:w0_split], w0[:, 0:w0_split]).then_inc(S("wqkvo_loaded"), 16)
            act.dma_start(W0s[:, w0_split:], w0[:, w0_split:]).then_inc(S("w0_loaded"), 16)

            def setup():
                nc.scalar.preload_act_table_set("natural_log_exp_and_others")
                act.wait_ge(S("group_loaded"), 16)
                deviations(0, 0, 1)
                act.wait_ge(S("cc_loaded"), 16)
                act.wait_ge(S("wqkvo_loaded"), 16)
                act.wait_ge(S("vpad_zero"), 1)
                act.wait_ge(S("borders_zero"), 6)

            def deviations(k, lo, hi):
                act.wait_ge(S("gnv_ready"), k + 1)
                af(gln[:, lo:hi, :], gnv[:, lo:hi, :], ACT.Ln, bias=wt("eps"), scale=-1.0).then_inc(S("gln_ready"), 1)
                act.wait_ge(S("gln_ready"), k + 1)
                af(grs[:, lo:hi, :], gln[:, lo:hi, :], ACT.Exp, scale=-0.5).then_inc(S("grs_ready"), 1)

            def front(b, j):
                yield 2
                act.wait_ge(S("qk_done"), b + 1)
                for i in range(2):
                    bias, src = wt("bqkvo", i, 1), F0[:, T * i:T * i + T]
                    af(e_qk[:, i, :], src, ACT.Exp, bias=bias)
                    af(r_qk[:, i, :], src, ACT.Relu, bias=bias).then_inc(S("qk_act"), 1)
                yield 8
                act.wait_ge(S("q_ready"), b + 1)
                af(Mq[:], wt("headq"), ACT.Copy, scale=qsum[:]).then_inc(S("mq_ready"), 1)
                yield 10
                act.wait_ge(S("vo_done"), b + 1)
                wait(act, "lepe_done", b)
                af(vpad[:, 0:WP * WP].rearrange("p (h w) -> p h w", h=WP)[:, PAD:PAD + H, PAD:PAD + W],
                   F0[:, 0:T].rearrange("p (h w) -> p h w", h=H),
                   ACT.Identity, bias=wt("bqkvo", 2, 1)).then_inc(S("vpad_ready"), 1)
                yield 10
                af(vS[:], F0[:, 0:T], ACT.Identity, bias=wt("bqkvo", 2, 1))
                yield 10
                wait(act, "u3_ready", b - 1)
                af(oS[j][:], F0[:, T:2 * T], ACT.Identity, bias=wt("bqkvo", 3, 1)).then_inc(S("o_ready"), 1)
                yield 14
                act.wait_ge(S("nmx_ready"), b + 1)
                af(Ex[:], F0[:, 0:T], ACT.Exp, bias=nmx[:], accum_out=sumE[:]).then_inc(S("exp_eff"), 1)
                yield 17
                act.wait_ge(S("kk_ready"), b + 1)
                af(Mk[:], wt("head"), ACT.Copy, scale=ksum[:]).then_inc(S("mk_ready"), 1)
                yield 20
                act.wait_ge(S("den_done"), b + 1)
                wait(act, "u1_ready", b - 1)
                af(lz[:], F0[:, 0:T], ACT.Ln, bias=wt("zeps")).then_inc(S("lz_ready"), 1)
                yield 28
                act.wait_ge(S("lz_ready"), b + 1)
                af(zS[j][:], lz[:], ACT.Exp, scale=-1.0).then_inc(S("zS_ready"), 1)
                yield 28
                act.wait_ge(S("kvT_done"), b + 1)
                nc.scalar.copy(flat(KVT[:]), F0[:]).then_inc(S("kvT_ready"), 1)

            def mid(b, j):
                yield 13
                act.wait_ge(S("x1_ready"), b + 1)
                af(x1sq[:].unsqueeze(1), X[:, bass.ds(b, 1), :], ACT.Square, accum_out=gi[:, 1:2]).then_inc(
                    S("gi_ready"), 1)
                yield 16
                act.wait_ge(S("nv_ready"), b + 1)
                af(lnv[:], nv[:], ACT.Ln, bias=wt("eps"), scale=-1.0).then_inc(S("lnv_ready"), 1)
                yield 16
                act.wait_ge(S("lnv_ready"), b + 1)
                af(rs[:], lnv[:], ACT.Exp, scale=-0.5).then_inc(S("rs_ready"), 1)
                yield 18
                act.wait_ge(S("xc_done"), b + 1)
                af(sq[:], F1[:, 0:T], ACT.Square).then_inc(S("sq_ready"), 1)
                yield 20
                act.wait_ge(S("var_done"), b + 1)
                af(lr[:], F1[:, T:2 * T], ACT.Ln, bias=wt("eps")).then_inc(S("lr_ready"), 1)
                yield 20
                act.wait_ge(S("lr_ready"), b + 1)
                af(rr[:], lr[:], ACT.Exp, scale=-0.5).then_inc(S("rr_ready"), 1)
                yield 23
                act.wait_ge(S("xl_ready"), b + 1)
                wait(act, "z_done", b)
                wait(act, "xk_ready", b - 1)
                af(XN[j][:, DCONV - 1:], xl[:], ACT.Identity, bias=wt("lnb")).then_inc(S("xn_ready"), 1)

            def tail(b, j):
                yield 4
                act.wait_ge(S("xp_done"), b + 1)
                wait(act, "y_summed", GROUPS * (b - 1))
                af(flat(xs[j][:]), F2[:], ACT.Silu, bias=wt("convb")).then_inc(S("xs_ready"), 1)
                act.wait_ge(S("z_done"), b + 1)
                wait(act, "y2_ready", b - 1)
                af(flat(zs[j][:]), F2[:], ACT.Silu).then_inc(S("zs_ready"), 1)
                nc.scalar.preload_act_table_set("natural_log_exp_and_others")
                yield 4
                act.wait_ge(S("dt_done"), b + 1)
                wait(act, "delta_ready", b)
                af(rl[:], F2[:], ACT.Relu, bias=wt("bdt"))
                af(ab[:], F2[:], ACT.Abs, bias=wt("bdt")).then_inc(S("abs_ready"), 1)
                yield 4
                act.wait_ge(S("abs_ready"), b + 1)
                af(em[:], ab[:], ACT.Exp, scale=-1.0).then_inc(S("em_ready"), 1)
                yield 5
                act.wait_ge(S("em_ready"), b + 1)
                wait(act, "cor_ready", b)
                af(um1[:], em[:], ACT.Identity, bias=1.0).then_inc(S("um1_ready"), 1)
                yield 5
                af(lnu[:], em[:], ACT.Ln, bias=1.0).then_inc(S("lnu_ready"), 1)
                yield 6
                act.wait_ge(S("bc_done"), b + 1)
                wait(act, "bc_copied", 16 * 2 * b)
                wait(act, "hc_ready", GROUPS * (b - 1))
                nc.scalar.copy(bc[:], F2[0:2 * 2 * DS, :]).then_inc(S("bc_ready"), 1)
                yield 9
                act.wait_ge(S("z_delta"), b + 1)
                wait(act, "regrouped", 16 * 4 * NPARTS * b)
                nc.scalar.copy(parts[0][:], Z[:]).then_inc(S("part0_ready"), 1)
                yield 14
                act.wait_ge(S("rem_ready"), b + 1)
                nc.scalar.copy(parts[1][:], Z[:]).then_inc(S("part1_ready"), 1)
                yield 16
                wait(act, "xc2_done", b - 1)
                af(xk[j][:], XN[j][:, DCONV - 1:], ACT.Copy, scale=wt("skip")).then_inc(S("xk_ready"), 1)

            def back(b, j):
                yield 23
                act.wait_ge(S("xc2_done"), b + 1)
                af(sq2[:], F3[:, 0:T], ACT.Square).then_inc(S("sq2_ready"), 1)
                yield 25
                act.wait_ge(S("var2_done"), b + 1)
                af(lr2[:], F3[:, T:2 * T], ACT.Ln, bias=wt("eps")).then_inc(S("lr2_ready"), 1)
                yield 25
                act.wait_ge(S("lr2_ready"), b + 1)
                af(rr2[:], lr2[:], ACT.Exp, scale=-0.5).then_inc(S("rr2_ready"), 1)

            def decay(u, g, half):
                if half == 0:
                    wait(act, "h_ready", u - 3)
                act.wait_ge(S("delta_bc"), 2 * u + half + 1)
                af(dec[g % 4][:, 2 * half:2 * half + 2, 1:T], D[:].rearrange("p (q t) -> p q t", q=2)[:, :, 1:T],
                   ACT.Exp, scale=negA[:, g:g + 1]).then_inc(S("decay_ready"), 1)

            def start():
                act.wait_ge(S("negA_ready"), 1)
                for g in range(LEAD):
                    for half in range(2):
                        decay(g, g, half)

            def unit(b, j, g, side, more):
                u, g2 = GROUPS * b + g + LEAD, (g + LEAD) % GROUPS
                for half in range(2):
                    side()
                    side()
                    if g + LEAD < GROUPS or more:
                        decay(u, g2, half)

            def weights(b, j):
                yield 10
                deviations(1, 1, B)
                yield 23
                act.wait_ge(S("w0_loaded"), 16)
                act.wait_ge(S("w1_loaded"), 32)
                af(negA0[:], wt("alog"), ACT.Exp).then_inc(S("expA"), 1)

            setup()
            periods(act, (weights, front, mid, tail, back), start, unit, lambda: None)

        @block.gpsimd
        def _(pool):
            tt = nc.gpsimd.tensor_tensor
            nc.gpsimd.memset(vpad[:], 0.0).then_inc(S("vpad_zero"), 1)
            for j in range(2):
                nc.gpsimd.memset(XN[j][:, 0:DCONV - 1], 0.0).then_inc(S("borders_zero"), 1)
            for tile in dec:
                nc.gpsimd.memset(tile[:, :, 0:1], 0.0).then_inc(S("borders_zero"), 1)
            pool.wait_ge(S("w0_loaded"), 16)

            def front(b, j):
                yield 20
                pool.wait_ge(S("kk_ready"), b + 1)
                tt(t1[:], QK[:], wt("cos").unsqueeze(1).broadcast_to([P, 2, T]), ALU.mult).then_inc(S("t1_ready"), 1)
                yield 22
                pool.wait_ge(S("t1_ready"), b + 1)
                pool.wait_ge(S("t2_ready"), b + 1)
                wait(pool, "res_done", b - 1)
                tt(QKR[j][:], t1[:], t2[:], ALU.add).then_inc(S("rope_ready"), 1)

            def mid(b, j):
                yield 10
                pool.wait_ge(S("u2_ready"), b + 1)
                pool.wait_ge(S("o_ready"), b + 1)
                tt(u3[:], u2[:], oS[j][:], ALU.mult).then_inc(S("u3_ready"), 1)

            def tail(b, j):
                yield 12
                pool.wait_ge(S("part0_ready"), b + 1)
                tt(Z[:], Z[:], parts[0][:], ALU.subtract).then_inc(S("rem_ready"), 1)
                yield 16
                pool.wait_ge(S("rem_ready"), b + 1)
                pool.wait_ge(S("part1_ready"), b + 1)
                tt(parts[2][:], Z[:], parts[1][:], ALU.subtract).then_inc(S("part2_ready"), 1)

            def back(b, j):
                yield from ()

            def unit(b, j, g, side, more):
                side()
                side()
                u = GROUPS * b + g
                pool.wait_ge(S("h_ready"), u + 1)
                if g == 0:
                    pool.wait_ge(S("bc_copied"), 16 * 2 * (b + 1))
                tt(hst[g % 4][:], hst[g % 4][:], flat(Cs[j][:]), ALU.mult).then_inc(S("hc_ready"), 1)
                side()
                side()

            def weights(b, j):
                yield from ()

            periods(pool, (weights, front, mid, tail, back), lambda: None, unit, lambda: None)

        @block.vector
        def _(dve):
            v = nc.vector

            def setup():
                statistics(0, 0, 1, F0)
                dve.wait_ge(S("cc_loaded"), 16)
                dve.wait_ge(S("borders_zero"), 6)

            def statistics(k, lo, hi, bank):
                for b in range(lo, hi):
                    dve.wait_ge(S(("x0_loaded", "x_loaded")[k]), 16)
                    v.bn_stats(gst[:, b, :], X[:, b, :]).then_inc(S("gst_ready"), 1)
                for b in range(lo, hi):
                    dve.wait_ge(S("gst_ready"), b + 1)
                    v.bn_aggr(gmv[:, b, :], gst[:, b, :]).then_inc(S("gmv_ready"), 1)
                dve.wait_ge(S("gmv_ready"), hi)
                means = gmv[:, lo:hi, 0:1]
                v.tensor_tensor(gsq[:, lo:hi, :], means, means, ALU.mult).then_inc(S("gsq_ready"), 1)
                v.tensor_copy(gin[:, lo:hi, 0:1], means)
                dve.wait_ge(S("gsq_ready"), 2 * k + 1)
                v.tensor_tensor(gin[:, lo:hi, 1:2], gsq[:, lo:hi, :], gmv[:, lo:hi, 1:2], ALU.add).then_inc(
                    S("gin_ready"), 1)
                dve.wait_ge(S("gavg_done"), k + 1)
                v.tensor_copy(gavg[:, lo:hi, :].rearrange("p b s -> p (b s)"), bank[:, 0:2 * (hi - lo)]).then_inc(
                    S("gavg_ready"), 1)
                dve.wait_ge(S("gavg_ready"), k + 1)
                averages = gavg[:, lo:hi, 0:1]
                v.tensor_tensor(gsq[:, lo:hi, :], averages, averages, ALU.mult).then_inc(S("gsq_ready"), 1)
                dve.wait_ge(S("gsq_ready"), 2 * k + 2)
                v.tensor_tensor(gnv[:, lo:hi, :], gsq[:, lo:hi, :], gavg[:, lo:hi, 1:2], ALU.subtract).then_inc(
                    S("gnv_ready"), 1)

            def weights(b, j):
                yield 0
                statistics(1, 1, B, F3)
                yield 8
                dve.wait_ge(S("w0_loaded"), 16)
                dve.wait_ge(S("w1_loaded"), 32)
                v.tensor_tensor(wpatch[:], wt("ident32").unsqueeze(1).broadcast_to([P, Q * ROUNDS, CM]),
                                wt("wlepe").unsqueeze(2).broadcast_to([P, Q * ROUNDS, CM]), ALU.mult)
                yield 11
                v.tensor_tensor(wtap[:], wt("wxp"), wt("convw"), ALU.mult)
                v.tensor_scalar(dsel[:].rearrange("p a m -> p (a m)"), wt("ident"), wt("D"), None, ALU.mult)
                yield 17
                v.tensor_copy(pick[:].rearrange("p a m -> p (a m)"), wt("pick")).then_inc(S("weights_ready"), 1)
                yield 24
                dve.wait_ge(S("wprod_done"), 1)
                v.tensor_tensor(wdt[:], F3[:, 0:P], wt("half"), ALU.mult)
                v.tensor_copy(flat(cwout[:]), F3[:, T:2 * T])
                v.tensor_tensor(bout[:], F3[:, P:P + 1], wt("pb"), ALU.add).then_inc(S("f3_read"), 1)
                yield 24
                dve.wait_ge(S("expA"), 1)
                v.tensor_scalar(negA[:], negA0[:], -1.0, None, ALU.mult).then_inc(S("negA_ready"), 1)

            def front(b, j):
                yield 1
                dve.wait_ge(S("grs_ready"), 1 if isinstance(b, int) and b == 0 else 2)
                wait(dve, "vo_done", b)
                v.tensor_scalar(xg0[:].unsqueeze(1), X[:, bass.ds(b, 1), :], gavg[:, bass.ds(b, 1), 0:1],
                                grs[:, bass.ds(b, 1), :], ALU.subtract, ALU.mult).then_inc(S("xg0_ready"), 1)
                yield 5
                dve.wait_ge(S("qk_act"), 2 * b + 2)
                v.scalar_tensor_tensor(out=QK[:, 0, :], in0=e_qk[:, 0, :], scalar=1.0, in1=r_qk[:, 0, :],
                                       op0=ALU.min, op1=ALU.add, accum_out=qsum[:]).then_inc(S("q_ready"), 1)
                yield 5
                v.scalar_tensor_tensor(out=kraw[:], in0=e_qk[:, 1, :], scalar=1.0, in1=r_qk[:, 1, :],
                                       op0=ALU.min, op1=ALU.add).then_inc(S("k_ready"), 1)
                yield 14
                dve.wait_ge(S("eff_done"), b + 1)
                v.tensor_reduce(nmx[:], F0[:, 0:T], AX_X, ALU.max, negate=True).then_inc(S("nmx_ready"), 1)
                yield 17
                dve.wait_ge(S("exp_eff"), b + 1)
                v.reciprocal(rE[:], sumE[:]).then_inc(S("rE_ready"), 1)
                yield 18
                dve.wait_ge(S("rE_ready"), b + 1)
                dve.wait_ge(S("k_ready"), b + 1)
                v.scalar_tensor_tensor(out=QK[:, 1, :], in0=Ex[:], scalar=rE[:], in1=kraw[:],
                                       op0=ALU.mult, op1=ALU.mult, accum_out=ksum[:]).then_inc(S("kk_ready"), 1)
                yield 20
                dve.wait_ge(S("w0_loaded"), 16)
                dve.wait_ge(S("rot_done"), b + 1)
                v.tensor_tensor(t2[:], F0[:].rearrange("p (a t) -> p a t", a=2),
                                wt("sin").unsqueeze(1).broadcast_to([P, 2, T]), ALU.mult).then_inc(S("t2_ready"), 1)
                yield 31
                dve.wait_ge(S("kv_done"), b + 1)
                wait(dve, "res_done", b - 1)
                v.tensor_tensor(KVM[j][:], F0[:, 0:P], wt("head"), ALU.mult).then_inc(S("kvm_ready"), 1)

            def mid(b, j):
                yield 10
                dve.wait_ge(S("res_done"), b + 1)
                dve.wait_ge(S("zS_ready"), b + 1)
                v.tensor_tensor(u1[:], F1[:, T:2 * T], zS[j][:], ALU.mult).then_inc(S("u1_ready"), 1)
                yield 11
                dve.wait_ge(S("lepe_done"), b + 1)
                dve.wait_ge(S("u1_ready"), b + 1)
                v.scalar_tensor_tensor(out=u2[:], in0=F1[:, 0:T], scalar=wt("blepe"), in1=u1[:],
                                       op0=ALU.add, op1=ALU.add).then_inc(S("u2_ready"), 1)
                yield 14
                dve.wait_ge(S("proj_done"), b + 1)
                xb = X[:, bass.ds(b, 1), :]
                v.scalar_tensor_tensor(out=xb, in0=F1[:, 0:T].unsqueeze(1), scalar=wt("bproj"), in1=xb,
                                       op0=ALU.add, op1=ALU.add, accum_out=gi[:, 0:1]).then_inc(S("x1_ready"), 1)
                yield 17
                dve.wait_ge(S("g2_done"), b + 1)
                v.tensor_copy(ga[:], F1[:, T:T + 2]).then_inc(S("ga_ready"), 1)
                yield 17
                dve.wait_ge(S("ga_ready"), b + 1)
                v.scalar_tensor_tensor(out=nv[:], in0=ga[:, 0:1], scalar=ga[:, 0:1], in1=ga[:, 1:2],
                                       op0=ALU.mult, op1=ALU.subtract).then_inc(S("nv_ready"), 1)
                yield 19
                dve.wait_ge(S("rs_ready"), b + 1)
                wait(dve, "xc_done", b)
                v.tensor_scalar(xg[:].unsqueeze(1), X[:, bass.ds(b, 1), :], ga[:, 0:1], rs[:], ALU.subtract,
                                ALU.mult).then_inc(S("xg_ready"), 1)
                yield 22
                dve.wait_ge(S("rr_ready"), b + 1)
                v.scalar_tensor_tensor(out=xl[:], in0=F1[:, 0:T], scalar=wt("lnw"), in1=rr[:],
                                       op0=ALU.mult, op1=ALU.mult).then_inc(S("xl_ready"), 1)

            def tail(b, j):
                yield 10
                dve.wait_ge(S("um1_ready"), b + 1)
                v.scalar_tensor_tensor(out=cor[:], in0=um1[:], scalar=1.0, in1=em[:],
                                       op0=ALU.subtract, op1=ALU.subtract).then_inc(S("cor_ready"), 1)
                yield 10
                dve.wait_ge(S("cor_ready"), b + 1)
                dve.wait_ge(S("lnu_ready"), b + 1)
                v.tensor_tensor(dl1[:], lnu[:], cor[:], ALU.subtract).then_inc(S("dl1_ready"), 1)
                yield 10
                dve.wait_ge(S("dl1_ready"), b + 1)
                wait(dve, "part2_ready", b)
                v.tensor_tensor(Z[:, 0, :], dl1[:], rl[:], ALU.add).then_inc(S("delta_ready"), 1)
                yield 11
                dve.wait_ge(S("delta_ready"), b + 1)
                v.tensor_tensor(Z[:, 1, :], Z[:, 0, :], flat(xs[j][:]), ALU.mult).then_inc(S("z_delta"), 1)

            def back(b, j):
                yield 4
                dve.wait_ge(S("y_summed"), GROUPS * (b + 1))
                v.tensor_tensor(flat(y2[:]), Y[:], flat(zs[j][:]), ALU.mult).then_inc(S("y2_ready"), 1)
                yield 27
                dve.wait_ge(S("rr2_ready"), b + 1)
                v.scalar_tensor_tensor(out=xl2[:], in0=F3[:, 0:T], scalar=wt("lnw"), in1=rr2[:],
                                       op0=ALU.mult, op1=ALU.mult).then_inc(S("xl2_ready"), 1)
                yield 31
                dve.wait_ge(S("proj2_done"), b + 1)
                xb = X[:, bass.ds(b, 1), :]
                v.scalar_tensor_tensor(out=xb, in0=F3[:, 0:T].unsqueeze(1), scalar=bout[:], in1=xb,
                                       op0=ALU.add, op1=ALU.add).then_inc(S("f3_read"), 1)

            def times_b(b, u, j, g):
                dve.wait_ge(S("du_bc"), u + 1)
                if g == 0:
                    dve.wait_ge(S("bc_copied"), 16 * 2 * (b + 1))
                wait(dve, "h_ready", u - 1)
                v.tensor_tensor(bin_[g % 2][:], flat(DU[:]), flat(Bs[j][:]), ALU.mult).then_inc(S("b_ready"), 1)

            def unit(b, j, g, side, more):
                u = GROUPS * b + g
                if g + 1 < GROUPS:
                    times_b(b, u + 1, j, g + 1)
                elif more:
                    times_b(b + 1, u + 1, 1 - j, 0)
                side()
                side()
                dve.wait_ge(S("b_ready"), u + 1)
                dve.wait_ge(S("decay_ready"), 2 * u + 2)
                wait(dve, "y_summed", u - 3)
                v.tensor_tensor_scan(hst[g % 4][:], flat(dec[g % 4][:]), bin_[g % 2][:], 0.0,
                                     ALU.mult, ALU.add).then_inc(S("h_ready"), 1)
                side()
                side()

            setup()
            periods(dve, (weights, front, mid, tail, back), lambda: times_b(0, 0, 0, 0), unit, lambda: None)


def kernel(**inputs):
    import numpy as np
    import concourse.bacc as bacc
    from concourse.bass_utils import run_bass_kernel_spmd as run

    a = {k: np.asarray(v) for k, v in inputs.items()}
    f = np.float32

    def pack(table, cols, named):
        out = np.zeros((P, cols), f)
        for name, block in named.items():
            start, width = table[name]
            out[:block.shape[0], start:start + width] = block.reshape(block.shape[0], width)
        return out

    def col(v):
        return v.reshape(-1, 1)

    wlepe = np.zeros((len(PATCH), CM, Q, ROUNDS), f)
    placed = set()
    for n, (py, px) in enumerate(PLACES):
        for k, (y, x) in enumerate(PATCH):
            tap = (py + y, px + x)
            if tap not in placed and 0 <= min(tap) and max(tap) < KS:
                placed.add(tap)
                wlepe[k, :, :, n] = a["L0_conv_w_lepe"][:, 0, tap[0], tap[1]].reshape(Q, CM).T
    wlepe = wlepe.reshape(P, Q * ROUNDS)

    w0 = pack(W0, W0_COLS, {
        "wqkvo": a["L0_conv_w_qkvo"].T, "bqkvo": a["L0_conv_b_qkvo"].reshape(4, C).T,
        "wlepe": wlepe, "blepe": col(a["L0_conv_b_lepe"]),
        "wproj": a["L0_conv_w_proj"].T, "bproj": col(a["L0_conv_b_proj"]),
        "cos": np.tile(a["L0_conv_cos"].T, (HEADS, 1)), "sin": np.tile(a["L0_conv_sin"].T, (HEADS, 1))})

    W_in, W_x, W_out = a["L1_conv_W_in"], a["L1_conv_W_x"], a["L1_conv_W_out"]
    wout = np.zeros((P, 2, P), f)
    wz = np.zeros((DCONV, CM, DI), f)
    wz[DCONV - 1] = W_in[DI:].T
    for kg in range(2):
        for q in range(Q):
            i = 2 * (q % 2) + q // 2
            wout[CM * q:CM * q + CM, kg, CM * i:CM * i + CM] = W_out[:, CM * kg:CM * kg + CM]
    wbc = np.zeros((2, DI, 2, 2 * DS), f)
    for half in range(2):
        wbc[half, :, half] = W_x[DTR:].T
    wbc = wbc.reshape(P, 2 * 2 * DS)
    both = lambda v: np.concatenate([v, v], 0)
    w1 = pack(W1, W1_COLS, {
        "lnw": col(a["L1_conv_norm_w"]), "lnb": col(a["L1_conv_norm_b"]), "wxp": np.tile(W_in[:DI].T, (DCONV, 1)),
        "wz": wz.reshape(P, DI),
        "convw": np.repeat(a["L1_conv_conv_w"][:, 0, :].T, CM, 0),
        "convb": col(both(a["L1_conv_conv_b"])),
        "wBC": wbc,
        "wdt_in": both(W_x[:DTR].T).T, "wdt_out": both(a["L1_conv_W_dt"]).T, "bdt": col(both(a["L1_conv_b_dt"])),
        "alog": a["L1_conv_A_log"].reshape(GROUPS, DD * DS).T, "D": col(both(a["L1_conv_D"])), "wout": wout,
        "pw": a["L1_conv_proj_w"].T, "pb": col(a["L1_conv_proj_b"]),
        "skip": np.broadcast_to(a["L1_conv_skip_scale"].reshape(1, 1), (P, 1))})

    c = np.arange(P)
    ident = np.eye(P, dtype=f)
    head = (c[:, None] // HD == c[None] // HD).astype(f)
    rot = np.zeros((P, P), f)
    rot[c[1::2], c[0::2]] = -1
    rot[c[0::2], c[1::2]] = 1
    pick = np.zeros((NPARTS, 32, 4, P), f)
    place = np.zeros((P, 4, CM), f)
    for s in range(4):
        place[c, s, DD * s + c // DS] = 1
        pick[:, DD * s + c // DS, s, c] = 1
    cc = pack(CC, CC_COLS, {
        "ident": ident, "head": head, "headq": head * f(HD ** -0.5 / T), "rot": rot,
        "group": (c[:, None] // 4 == c[None] // 4).astype(f) / 4,
        "groupsum": (c[:, None] // 4 == c[None] // 4).astype(f) / (4 * T), "center": ident - f(1 / C),
        "mean": np.full((P, P), 1 / C, f), "zeps": np.full((P, 1), 1e-6, f),
        "half": (c[:, None] // DI == c[None] // DI).astype(f), "eps": np.full((P, 1), LN_EPS, f),
        "ident32": ident[:, :CM] + ident[:, CM:2 * CM] + ident[:, 2 * CM:3 * CM] + ident[:, 3 * CM:],
        "pick": pick.reshape(NPARTS * 32, 4 * P), "place": place})

    nc = bacc.Bacc("TRN2", target_bir_lowering=False, num_devices=1)
    arrays, args = {}, []
    for name, v in (("x", a["x"]), ("w0", w0), ("w1", w1), ("cc", cc)):
        arrays[name] = np.ascontiguousarray(v)
        args.append(nc.dram_tensor(name, v.shape, mybir.dt.from_np(v.dtype), kind="ExternalInput").ap())
    out = nc.dram_tensor("out", (B, C, H, W), F32, kind="ExternalOutput").ap()
    block_kernel(nc, *args, out)
    r = run(nc, [arrays], core_ids=[0])
    return r.results[0]["out"]
```
